# Optimizing a Trainium2 kernel written in Bass

```python
import numpy as np
import jax
import jax.numpy as jnp

def _softmax(x, axis=-1):
    return jax.nn.softmax(x, axis=axis)

def _gelu(x):
    return jax.nn.gelu(x, approximate=True)

def _silu(x):
    return jax.nn.silu(x)

def _sigmoid(x):
    return jax.nn.sigmoid(x)

def _layernorm(x, axis=-1, eps=1e-05):
    m = jnp.mean(x, axis=axis, keepdims=True)
    v = jnp.var(x, axis=axis, keepdims=True)
    return (x - m) / jnp.sqrt(v + eps)

def _scatter_add(tgt, idx, src, axis=0):
    return tgt.at[idx].add(src)

def _segment_sum(src, seg, n):
    return jax.ops.segment_sum(src, seg, n)
kernel_name = 'mk_conv_preact_d2_conv_nchw32_r4_d6d470'

def setup_inputs(seed: int=0):
    np.random.seed(seed)
    _w = jnp.asarray

    def _rec_inputs():
        import jax
        import jax.numpy as jnp
        _gk = jax.random.key(seed)
        x = -0.0003929 + 0.9999 * jax.random.normal(jax.random.fold_in(_gk, 1), (8, 32, 64, 64), jnp.float32)
        return x
    x = _rec_inputs()

    def _L0_conv_setup():
        import jax, jax.numpy as jnp
        from jax import lax
        import numpy as np
        IN_CH, FEAT, OUT_CH = (32, 16, 32)

        def _lstm_scan(y, W_ih, W_hh, b_ih, b_hh):
            H = W_hh.shape[1]
            gx = jnp.einsum('nfc,gc->nfg', y, W_ih) + b_ih + b_hh
            gx = jnp.swapaxes(gx, 0, 1)

            def step(carry, g_in):
                h, c = carry
                g = g_in + h @ W_hh.T
                i, f, gg, o = jnp.split(g, 4, axis=-1)
                i = jax.nn.sigmoid(i)
                f = jax.nn.sigmoid(f)
                gg = jnp.tanh(gg)
                o = jax.nn.sigmoid(o)
                c = f * c + i * gg
                h = o * jnp.tanh(c)
                return ((h, c), h)
            N = y.shape[0]
            h0 = jnp.zeros((N, H), dtype=y.dtype)
            (_, _), hs = lax.scan(step, (h0, h0), gx)
            return jnp.swapaxes(hs, 0, 1)

        def _forward(x, W_ih_f, W_hh_f, b_ih_f, b_hh_f, W_ih_b, W_hh_b, b_ih_b, b_hh_b, W_lin, b_lin):
            b, c, f, t = x.shape
            y = jnp.transpose(x, (0, 3, 2, 1)).reshape(b * t, f, c).astype(jnp.float32)
            h_fwd = _lstm_scan(y, W_ih_f, W_hh_f, b_ih_f, b_hh_f)
            h_bwd = _lstm_scan(y[:, ::-1, :], W_ih_b, W_hh_b, b_ih_b, b_hh_b)[:, ::-1, :]
            h = jnp.concatenate([h_fwd, h_bwd], axis=-1)
            out = jnp.einsum('nfh,oh->nfo', h, W_lin) + b_lin
            out = out.reshape(b, t, f, -1)
            return jnp.transpose(out, (0, 3, 2, 1))
        key = jax.random.key(seed)
        ks = jax.random.split(key, 12)
        s = 0.05
        inp = {'x': jax.random.normal(ks[0], (8, 32, 64, 64), dtype=jnp.float32), 'W_ih_f': jax.random.normal(ks[1], (4 * FEAT, IN_CH), dtype=jnp.float32) * s, 'W_hh_f': jax.random.normal(ks[2], (4 * FEAT, FEAT), dtype=jnp.float32) * s, 'b_ih_f': jax.random.normal(ks[3], (4 * FEAT,), dtype=jnp.float32) * s, 'b_hh_f': jax.random.normal(ks[4], (4 * FEAT,), dtype=jnp.float32) * s, 'W_ih_b': jax.random.normal(ks[5], (4 * FEAT, IN_CH), dtype=jnp.float32) * s, 'W_hh_b': jax.random.normal(ks[6], (4 * FEAT, FEAT), dtype=jnp.float32) * s, 'b_ih_b': jax.random.normal(ks[7], (4 * FEAT,), dtype=jnp.float32) * s, 'b_hh_b': jax.random.normal(ks[8], (4 * FEAT,), dtype=jnp.float32) * s, 'W_lin': jax.random.normal(ks[9], (OUT_CH, 2 * FEAT), dtype=jnp.float32) * s, 'b_lin': jax.random.normal(ks[10], (OUT_CH,), dtype=jnp.float32) * s}
        return inp
    _L0_conv_all = _L0_conv_setup()
    _L0_conv_in = {k: v for k, v in _L0_conv_all.items() if k in ('W_ih_f', 'W_hh_f', 'b_ih_f', 'b_hh_f', 'W_ih_b', 'W_hh_b', 'b_ih_b', 'b_hh_b', 'W_lin', 'b_lin')}
    del _L0_conv_all

    def _L1_conv_setup():
        import jax, jax.numpy as jnp
        import numpy as np
        from jax import lax
        B, C, O, K, H, W = (4, 32, 32, 9, 64, 64)
        EPS = 1e-05

        def conv2d(x, w, b=None, stride=1, padding=1, groups=1):
            out = lax.conv_general_dilated(x, w, (stride, stride), [(padding, padding)] * 2, dimension_numbers=('NCHW', 'OIHW', 'NCHW'), feature_group_count=groups)
            if b is not None:
                out = out + b[None, :, None, None]
            return out

        def batchnorm(x, g, b):
            mean = jnp.mean(x, axis=(0, 2, 3), keepdims=True)
            var = jnp.var(x, axis=(0, 2, 3), keepdims=True)
            return (x - mean) * lax.rsqrt(var + EPS) * g[None, :, None, None] + b[None, :, None, None]

        def grid_sample_zeros(img, ix, iy):
            Bi, Ci, Hi, Wi = img.shape
            x0 = jnp.floor(ix)
            y0 = jnp.floor(iy)
            x1 = x0 + 1.0
            y1 = y0 + 1.0
            wx1 = ix - x0
            wx0 = 1.0 - wx1
            wy1 = iy - y0
            wy0 = 1.0 - wy1
            imgf = img.reshape(Bi, Ci, Hi * Wi)

            def corner(xc, yc, w):
                valid = (xc >= 0) & (xc <= Wi - 1) & (yc >= 0) & (yc <= Hi - 1)
                xi = jnp.clip(xc, 0, Wi - 1).astype(jnp.int32)
                yi = jnp.clip(yc, 0, Hi - 1).astype(jnp.int32)
                idx = yi * Wi + xi
                vals = jax.vmap(lambda im, id_: im[:, id_])(imgf, idx)
                return vals * (w * valid.astype(w.dtype))[:, None]
            return corner(x0, y0, wx0 * wy0) + corner(x1, y0, wx1 * wy0) + corner(x0, y1, wx0 * wy1) + corner(x1, y1, wx1 * wy1)

        def dsc_axis(x, offset, weight, axis):
            Bi, Ci, Hi, Wi = x.shape
            off = jnp.transpose(offset, (0, 2, 3, 1))
            hb = jnp.arange(Hi, dtype=x.dtype)[None, :, None, None]
            wb = jnp.arange(Wi, dtype=x.dtype)[None, None, :, None]
            if axis == 'x':
                ix = wb + off
                iy = jnp.broadcast_to(hb, off.shape)
            else:
                iy = hb + off
                ix = jnp.broadcast_to(wb, off.shape)
            s = grid_sample_zeros(x, ix, iy)
            return jnp.einsum('bchwk,ock->bohw', s, weight)

        def offset_branch(x, dw_w, dw_b, bn_g, bn_b, pw_w, pw_b):
            h = conv2d(x, dw_w, dw_b, padding=1, groups=x.shape[1])
            h = jax.nn.relu(batchnorm(h, bn_g, bn_b))
            return conv2d(h, pw_w, pw_b, padding=0)
        key = jax.random.key(seed)
        ks = jax.random.split(key, 16)
        n = lambda k, sh, s: jax.random.normal(k, sh, dtype=jnp.float32) * s
        d = {}
        d['x'] = n(ks[0], (B, C, H, W), 1.0)
        d['conv_w'] = n(ks[1], (O, C, 3, 3), (2.0 / (C * 9)) ** 0.5)
        d['conv_b'] = jnp.zeros((O,), jnp.float32)
        d['offx_dw_w'] = n(ks[2], (C, 1, 3, 3), 0.3)
        d['offx_dw_b'] = jnp.zeros((C,), jnp.float32)
        d['offx_bn_g'] = jnp.ones((C,), jnp.float32)
        d['offx_bn_b'] = jnp.zeros((C,), jnp.float32)
        d['offx_pw_w'] = n(ks[3], (K, C, 1, 1), 0.1)
        d['offx_pw_b'] = n(ks[4], (K,), 0.1)
        d['offy_dw_w'] = n(ks[5], (C, 1, 3, 3), 0.3)
        d['offy_dw_b'] = jnp.zeros((C,), jnp.float32)
        d['offy_bn_g'] = jnp.ones((C,), jnp.float32)
        d['offy_bn_b'] = jnp.zeros((C,), jnp.float32)
        d['offy_pw_w'] = n(ks[6], (K, C, 1, 1), 0.1)
        d['offy_pw_b'] = n(ks[7], (K,), 0.1)
        d['dscx_w'] = n(ks[8], (O, C, K), (2.0 / (C * K)) ** 0.5)
        d['dscy_w'] = n(ks[9], (O, C, K), (2.0 / (C * K)) ** 0.5)
        d['fus_w'] = n(ks[10], (O, 3 * O, 1, 1), (2.0 / (3 * O)) ** 0.5)
        d['fus_bn_g'] = jnp.ones((O,), jnp.float32)
        d['fus_bn_b'] = jnp.zeros((O,), jnp.float32)
        return d
    _L1_conv_all = _L1_conv_setup()
    _L1_conv_in = {k: v for k, v in _L1_conv_all.items() if k in ('conv_w', 'conv_b', 'offx_dw_w', 'offx_dw_b', 'offx_bn_g', 'offx_bn_b', 'offx_pw_w', 'offx_pw_b', 'offy_dw_w', 'offy_dw_b', 'offy_bn_g', 'offy_bn_b', 'offy_pw_w', 'offy_pw_b', 'dscx_w', 'dscy_w', 'fus_w', 'fus_bn_g', 'fus_bn_b')}
    del _L1_conv_all
    return {'x': x, 'L0_conv_W_ih_f': _L0_conv_in['W_ih_f'], 'L0_conv_W_hh_f': _L0_conv_in['W_hh_f'], 'L0_conv_b_ih_f': _L0_conv_in['b_ih_f'], 'L0_conv_b_hh_f': _L0_conv_in['b_hh_f'], 'L0_conv_W_ih_b': _L0_conv_in['W_ih_b'], 'L0_conv_W_hh_b': _L0_conv_in['W_hh_b'], 'L0_conv_b_ih_b': _L0_conv_in['b_ih_b'], 'L0_conv_b_hh_b': _L0_conv_in['b_hh_b'], 'L0_conv_W_lin': _L0_conv_in['W_lin'], 'L0_conv_b_lin': _L0_conv_in['b_lin'], 'L1_conv_conv_w': _L1_conv_in['conv_w'], 'L1_conv_conv_b': _L1_conv_in['conv_b'], 'L1_conv_offx_dw_w': _L1_conv_in['offx_dw_w'], 'L1_conv_offx_dw_b': _L1_conv_in['offx_dw_b'], 'L1_conv_offx_bn_g': _L1_conv_in['offx_bn_g'], 'L1_conv_offx_bn_b': _L1_conv_in['offx_bn_b'], 'L1_conv_offx_pw_w': _L1_conv_in['offx_pw_w'], 'L1_conv_offx_pw_b': _L1_conv_in['offx_pw_b'], 'L1_conv_offy_dw_w': _L1_conv_in['offy_dw_w'], 'L1_conv_offy_dw_b': _L1_conv_in['offy_dw_b'], 'L1_conv_offy_bn_g': _L1_conv_in['offy_bn_g'], 'L1_conv_offy_bn_b': _L1_conv_in['offy_bn_b'], 'L1_conv_offy_pw_w': _L1_conv_in['offy_pw_w'], 'L1_conv_offy_pw_b': _L1_conv_in['offy_pw_b'], 'L1_conv_dscx_w': _L1_conv_in['dscx_w'], 'L1_conv_dscy_w': _L1_conv_in['dscy_w'], 'L1_conv_fus_w': _L1_conv_in['fus_w'], 'L1_conv_fus_bn_g': _L1_conv_in['fus_bn_g'], 'L1_conv_fus_bn_b': _L1_conv_in['fus_bn_b']}

def reference(x, L0_conv_W_ih_f, L0_conv_W_hh_f, L0_conv_b_ih_f, L0_conv_b_hh_f, L0_conv_W_ih_b, L0_conv_W_hh_b, L0_conv_b_ih_b, L0_conv_b_hh_b, L0_conv_W_lin, L0_conv_b_lin, L1_conv_conv_w, L1_conv_conv_b, L1_conv_offx_dw_w, L1_conv_offx_dw_b, L1_conv_offx_bn_g, L1_conv_offx_bn_b, L1_conv_offx_pw_w, L1_conv_offx_pw_b, L1_conv_offy_dw_w, L1_conv_offy_dw_b, L1_conv_offy_bn_g, L1_conv_offy_bn_b, L1_conv_offy_pw_w, L1_conv_offy_pw_b, L1_conv_dscx_w, L1_conv_dscy_w, L1_conv_fus_w, L1_conv_fus_bn_g, L1_conv_fus_bn_b):
    import jax
    import jax.numpy as jnp

    def _L0_conv_ref(x, W_ih_f, W_hh_f, b_ih_f, b_hh_f, W_ih_b, W_hh_b, b_ih_b, b_hh_b, W_lin, b_lin):
        import jax, jax.numpy as jnp
        from jax import lax
        import numpy as np
        IN_CH, FEAT, OUT_CH = (32, 16, 32)

        def _lstm_scan(y, W_ih, W_hh, b_ih, b_hh):
            H = W_hh.shape[1]
            gx = jnp.einsum('nfc,gc->nfg', y, W_ih) + b_ih + b_hh
            gx = jnp.swapaxes(gx, 0, 1)

            def step(carry, g_in):
                h, c = carry
                g = g_in + h @ W_hh.T
                i, f, gg, o = jnp.split(g, 4, axis=-1)
                i = jax.nn.sigmoid(i)
                f = jax.nn.sigmoid(f)
                gg = jnp.tanh(gg)
                o = jax.nn.sigmoid(o)
                c = f * c + i * gg
                h = o * jnp.tanh(c)
                return ((h, c), h)
            N = y.shape[0]
            h0 = jnp.zeros((N, H), dtype=y.dtype)
            (_, _), hs = lax.scan(step, (h0, h0), gx)
            return jnp.swapaxes(hs, 0, 1)

        def _forward(x, W_ih_f, W_hh_f, b_ih_f, b_hh_f, W_ih_b, W_hh_b, b_ih_b, b_hh_b, W_lin, b_lin):
            b, c, f, t = x.shape
            y = jnp.transpose(x, (0, 3, 2, 1)).reshape(b * t, f, c).astype(jnp.float32)
            h_fwd = _lstm_scan(y, W_ih_f, W_hh_f, b_ih_f, b_hh_f)
            h_bwd = _lstm_scan(y[:, ::-1, :], W_ih_b, W_hh_b, b_ih_b, b_hh_b)[:, ::-1, :]
            h = jnp.concatenate([h_fwd, h_bwd], axis=-1)
            out = jnp.einsum('nfh,oh->nfo', h, W_lin) + b_lin
            out = out.reshape(b, t, f, -1)
            return jnp.transpose(out, (0, 3, 2, 1))
        return _forward(x, W_ih_f, W_hh_f, b_ih_f, b_hh_f, W_ih_b, W_hh_b, b_ih_b, b_hh_b, W_lin, b_lin)

    def _L1_conv_ref(x, conv_w, conv_b, offx_dw_w, offx_dw_b, offx_bn_g, offx_bn_b, offx_pw_w, offx_pw_b, offy_dw_w, offy_dw_b, offy_bn_g, offy_bn_b, offy_pw_w, offy_pw_b, dscx_w, dscy_w, fus_w, fus_bn_g, fus_bn_b):
        import jax, jax.numpy as jnp
        import numpy as np
        from jax import lax
        B, C, O, K, H, W = (4, 32, 32, 9, 64, 64)
        EPS = 1e-05

        def conv2d(x, w, b=None, stride=1, padding=1, groups=1):
            out = lax.conv_general_dilated(x, w, (stride, stride), [(padding, padding)] * 2, dimension_numbers=('NCHW', 'OIHW', 'NCHW'), feature_group_count=groups)
            if b is not None:
                out = out + b[None, :, None, None]
            return out

        def batchnorm(x, g, b):
            mean = jnp.mean(x, axis=(0, 2, 3), keepdims=True)
            var = jnp.var(x, axis=(0, 2, 3), keepdims=True)
            return (x - mean) * lax.rsqrt(var + EPS) * g[None, :, None, None] + b[None, :, None, None]

        def grid_sample_zeros(img, ix, iy):
            Bi, Ci, Hi, Wi = img.shape
            x0 = jnp.floor(ix)
            y0 = jnp.floor(iy)
            x1 = x0 + 1.0
            y1 = y0 + 1.0
            wx1 = ix - x0
            wx0 = 1.0 - wx1
            wy1 = iy - y0
            wy0 = 1.0 - wy1
            imgf = img.reshape(Bi, Ci, Hi * Wi)

            def corner(xc, yc, w):
                valid = (xc >= 0) & (xc <= Wi - 1) & (yc >= 0) & (yc <= Hi - 1)
                xi = jnp.clip(xc, 0, Wi - 1).astype(jnp.int32)
                yi = jnp.clip(yc, 0, Hi - 1).astype(jnp.int32)
                idx = yi * Wi + xi
                vals = jax.vmap(lambda im, id_: im[:, id_])(imgf, idx)
                return vals * (w * valid.astype(w.dtype))[:, None]
            return corner(x0, y0, wx0 * wy0) + corner(x1, y0, wx1 * wy0) + corner(x0, y1, wx0 * wy1) + corner(x1, y1, wx1 * wy1)

        def dsc_axis(x, offset, weight, axis):
            Bi, Ci, Hi, Wi = x.shape
            off = jnp.transpose(offset, (0, 2, 3, 1))
            hb = jnp.arange(Hi, dtype=x.dtype)[None, :, None, None]
            wb = jnp.arange(Wi, dtype=x.dtype)[None, None, :, None]
            if axis == 'x':
                ix = wb + off
                iy = jnp.broadcast_to(hb, off.shape)
            else:
                iy = hb + off
                ix = jnp.broadcast_to(wb, off.shape)
            s = grid_sample_zeros(x, ix, iy)
            return jnp.einsum('bchwk,ock->bohw', s, weight)

        def offset_branch(x, dw_w, dw_b, bn_g, bn_b, pw_w, pw_b):
            h = conv2d(x, dw_w, dw_b, padding=1, groups=x.shape[1])
            h = jax.nn.relu(batchnorm(h, bn_g, bn_b))
            return conv2d(h, pw_w, pw_b, padding=0)
        out_standard = conv2d(x, conv_w, conv_b, padding=1)
        offset_x = offset_branch(x, offx_dw_w, offx_dw_b, offx_bn_g, offx_bn_b, offx_pw_w, offx_pw_b)
        offset_y = offset_branch(x, offy_dw_w, offy_dw_b, offy_bn_g, offy_bn_b, offy_pw_w, offy_pw_b)
        out_x = dsc_axis(x, offset_x, dscx_w, 'x')
        out_y = dsc_axis(x, offset_y, dscy_w, 'y')
        out = jnp.concatenate([out_standard, out_x, out_y], axis=1)
        out = conv2d(out, fus_w, None, padding=0)
        return jax.nn.relu(batchnorm(out, fus_bn_g, fus_bn_b))

    def _gn(v, G=16, eps=1e-05):
        B_, C_, H_, W_ = v.shape
        g = v.reshape(B_, G, C_ // G, H_, W_)
        m = jnp.mean(g, axis=(2, 3, 4), keepdims=True)
        s = jnp.var(g, axis=(2, 3, 4), keepdims=True)
        return ((g - m) / jnp.sqrt(s + eps)).reshape(v.shape)

    def _ln_c(v, eps=1e-06):
        m = jnp.mean(v, axis=1, keepdims=True)
        s = jnp.var(v, axis=1, keepdims=True)
        return (v - m) / jnp.sqrt(s + eps)

    def _ln_t(v, eps=1e-05):
        m = jnp.mean(v, axis=-1, keepdims=True)
        s = jnp.var(v, axis=-1, keepdims=True)
        return (v - m) / jnp.sqrt(s + eps)

    def _to_tokens(v):
        B_, C_, H_, W_ = v.shape
        return v.reshape(B_, C_, H_ * W_).transpose(0, 2, 1)

    def _from_tokens(t, like):
        B_, C_, H_, W_ = like.shape
        return t.transpose(0, 2, 1).reshape(B_, C_, H_, W_)
    x = x + _L0_conv_ref(_gn(x), L0_conv_W_ih_f, L0_conv_W_hh_f, L0_conv_b_ih_f, L0_conv_b_hh_f, L0_conv_W_ih_b, L0_conv_W_hh_b, L0_conv_b_ih_b, L0_conv_b_hh_b, L0_conv_W_lin, L0_conv_b_lin)
    x = x + _L1_conv_ref(_gn(x), L1_conv_conv_w, L1_conv_conv_b, L1_conv_offx_dw_w, L1_conv_offx_dw_b, L1_conv_offx_bn_g, L1_conv_offx_bn_b, L1_conv_offx_pw_w, L1_conv_offx_pw_b, L1_conv_offy_dw_w, L1_conv_offy_dw_b, L1_conv_offy_bn_g, L1_conv_offy_bn_b, L1_conv_offy_pw_w, L1_conv_offy_pw_b, L1_conv_dscx_w, L1_conv_dscy_w, L1_conv_fus_w, L1_conv_fus_bn_g, L1_conv_fus_bn_b)
    return x

_drawn_inputs = setup_inputs


def setup_inputs(seed=0):
    import zlib

    import numpy as np

    out = dict(_drawn_inputs(seed))
    spreads = {'L1_conv_conv_b': (0.0, 2.0),
     'L1_conv_offx_dw_b': (0.0, 2.0),
     'L1_conv_offx_bn_g': (1.0, 0.2),
     'L1_conv_offx_bn_b': (0.0, 0.438),
     'L1_conv_offy_dw_b': (0.0, 2.0),
     'L1_conv_offy_bn_g': (1.0, 0.2),
     'L1_conv_offy_bn_b': (0.0, 0.361),
     'L1_conv_fus_bn_g': (1.0, 0.2),
     'L1_conv_fus_bn_b': (0.0, 0.1)}
    factors = {'L0_conv_W_ih_f': 3.144,
     'L0_conv_W_hh_f': 22.101,
     'L0_conv_b_ih_f': 8.0,
     'L0_conv_b_hh_f': 8.0,
     'L0_conv_W_ih_b': 3.801,
     'L0_conv_W_hh_b': 26.554,
     'L0_conv_b_ih_b': 8.0,
     'L0_conv_b_hh_b': 26.999}
    for name, (base, spread) in spreads.items():
        noise = np.random.default_rng([zlib.crc32(name.encode()), seed]).standard_normal(out[name].shape)
        drawn = base * np.exp(spread * noise) if base else spread * noise
        out[name] = jnp.asarray(drawn.astype(out[name].dtype))
    for name, factor in factors.items():
        out[name] = (out[name] * factor).astype(out[name].dtype)
    return out
```

```python
import concourse.bass as bass
from concourse import mybir
from contextlib import ExitStack

F32 = mybir.dt.float32
BF16 = mybir.dt.bfloat16
P = 128
Q = 4
C = 32
S = 64
PIX = S * S
L = 2 * PIX
HID = 16
K = 9
SEQ = 2 * S
ROWS = 8
CH = ROWS * S
NCH = L // CH
PAD = S + 2
PARTS = 3
NOFF = Q * K
ONE_ROW = PARTS * NOFF
NROW = ONE_ROW + 2
HROWS = ROWS // 2
SL = HROWS * S
NSEL = Q * 4 + 2
GN_EPS = 1e-5
BN_EPS = 1e-5
GN1, GN2, BNX, BNY, BNF = range(5)

(V_BLIN, V_CONVB, V_FG, V_FB, V_G1, V_G2) = range(6)
V_DWB, V_BNG, V_BNB, V_PWB = 6, 8, 10, 12
V_DW = 14
NVEC = V_DW + 18


def build(nc, x, wx, whh, wlin, gate_bias, gate_ind, cw, fus, dsc, pw, dm, vec, avg, sel, pos, out):
    ACT = mybir.ActivationFunctionType
    ALU = mybir.AluOpType
    AX = mybir.AxisListType
    ds = bass.ds
    ctx = ExitStack()
    with ctx:
        def sb(name, shape, dt=F32):
            return ctx.enter_context(nc.sbuf_tensor(name, shape, dt))

        def sem(name):
            return ctx.enter_context(nc.semaphore(name))

        xs = sb("xs", [P, L])
        img = sb("img", [P, 2 * PAD * PAD])
        seq = sb("seq", [P, (S + 1) * SEQ])
        wide = sb("wide", [P, 2 * L])
        offs = sb("offs", [P, 2 * L], BF16)
        wc = sb("wc", [P, 2, K * C])
        vecs = sb("vecs", [P, NVEC])
        avgs = sb("avgs", [P, 2, P])
        sels = sb("sels", [NROW, NSEL, P], BF16)
        pws = sb("pws", [P, 2, NROW])
        y8 = sb("y8", [P, 2, Q, HROWS, C])
        stats = sb("stats", [P, NCH, 6])
        small = sb("small", [P, 41])
        mv = small[:, 0:4].rearrange("p (n a) -> p n a", a=2)
        nt = small[:, 4:20].rearrange("p (a n) -> p a n", n=2)
        coef = small[:, 20:40].rearrange("p (i a n) -> p i a n", a=2, n=2)
        cbias = small[:, 40:41]
        psum = ctx.enter_context(nc.psum_tensor("psum", [P, 8 * CH], F32))
        ps = [psum[:, i * CH:(i + 1) * CH] for i in range(8)]

        xv = xs[:, :].rearrange("p (b f t) -> p b f t", b=2, f=S)
        xg = img[:, 0:L].rearrange("p (b f t) -> p b f t", b=2, f=S)
        pad = img[:, :].rearrange("p (b h w) -> p b h w", b=2, h=PAD)
        acc = seq[:, 0:L]
        accv = acc.rearrange("p (b h w) -> p b h w", b=2, h=S)

        o = 0
        def region(n):
            nonlocal o
            o += n
            return wide[:, o - n:o]
        wx_s = region(2 * 4 * P).rearrange("p (d g m) -> p d g m", d=2, g=4)
        whh_s = region(4 * P).rearrange("p (g m) -> p g m", g=4)
        wlin_s = region(2 * P).rearrange("p (d m) -> p d m", d=2)
        gb_f = region(2 * P)[0:12, :].rearrange("p (a m) -> p a m", a=2)
        gb_r = region(P)[0:12, :]
        gb_1 = region(P // 2)[0:12, :].bitcast(BF16)
        gb_2 = region(P // 2)[0:12, :].bitcast(BF16)
        gb_b = region(P // 2)[0:12, :].bitcast(BF16)
        gi_b = region(CH // 2)[0:12, :].bitcast(BF16)
        gc = region(2 * P)
        sif = region(2 * P)
        prod = region(2 * P)
        so = region(P)
        tc_ = region(P)
        dsc_s = region(2 * K * P)[0:C, :].rearrange("p (a k m) -> p a k m", a=2, k=K)
        f23_s = region(3 * C)[0:C, :].rearrange("p (a m) -> p a m", a=3)
        assert o <= 2 * L
        h_x = wide[:, 0:L]
        h_y = wide[:, L:2 * L]
        hxv = h_x.rearrange("p (b h w) -> p b h w", b=2, h=S)
        hyv = h_y.rearrange("p (b h w) -> p b h w", b=2, h=S)
        hv = (hxv, hyv)

        o = 0
        vt = region(2 * 4 * Q * SL).rearrange("p (a k q n) -> p a k q n", a=2, k=4, q=Q)
        v8 = region(2 * 2 * SL).rearrange("p (a q n) -> p a q n", a=2, q=2)
        yt = region(2 * Q * HROWS * P).rearrange("p (a q r m) -> p a q r m", a=2, q=Q, r=HROWS)
        xc = region(2 * SL).rearrange("p (a n) -> p a n", a=2)
        wm = region(2 * Q * K * C).rearrange("p (a q n) -> p a q n", a=2, q=Q)
        assert o <= 2 * L
        fin = h_y

        of = offs[:, :].bitcast(F32)
        cw_s = of[:, 0:K * P].rearrange("p (k m) -> p k m", k=K)
        cwf = of[:, K * P:2 * K * P].rearrange("p (k m) -> p k m", k=K)
        fus_s = of[:, 2 * K * P:2 * K * P + P]
        dmask = seq[0:ONE_ROW + 1, L:L + NROW].bitcast(BF16).rearrange("p (a n) -> p a n", a=2)
        ob = [offs[:, a * L:(a + 1) * L] for a in range(2)]

        x_in = sem("x_in"); lstm_in = sem("lstm_in"); conv_in = sem("conv_in"); misc_in = sem("misc_in")
        pos_in = sem("pos_in"); dmask_in = sem("dmask_in"); act_turn = sem("act_turn"); stored = sem("stored")
        mean_in = sem("mean_in"); mean_out = sem("mean_out"); dev_in = sem("dev_in")
        var_out = sem("var_out"); sqrt_in = sem("sqrt_in"); sqrt_out = sem("sqrt_out")
        norm_done = sem("norm_done"); link = sem("link")
        xg_ready = sem("xg_ready"); gb_ready = sem("gb_ready")
        gif_ready = sem("gif_ready"); o_ready = sem("o_ready"); sif_ready = sem("sif_ready")
        prod_ready = sem("prod_ready"); c_ready = sem("c_ready"); tc_ready = sem("tc_ready")
        h_ready = sem("h_ready"); lin_ready = sem("lin_ready"); x1_ready = sem("x1_ready")
        fuse_mm = sem("fuse_mm"); zeroed = sem("zeroed"); fuse_ev = sem("fuse_ev"); pool_chain = sem("pool_chain")
        pad_zero = sem("pad_zero"); pad_ready = sem("pad_ready");
        conv_mm = sem("conv_mm"); conv_ev = sem("conv_ev")
        dw_done = sem("dw_done"); relu_done = sem("relu_done")
        off_mm = sem("off_mm"); part1 = sem("part1"); rest1 = sem("rest1")
        part2 = sem("part2"); rest2 = sem("rest2"); part3 = sem("part3"); rows_set = sem("rows_set")
        wm_zero = sem("wm_zero"); wm_ready = sem("wm_ready"); y8_zero = sem("y8_zero")
        xc_ready = sem("xc_ready"); d_ready = sem("d_ready"); d_read = sem("d_read"); v_ready = sem("v_ready")
        y_ready = sem("y_ready"); y_read = sem("y_read"); y8_ready = sem("y8_ready"); y8_read = sem("y8_read")
        out_ready = sem("out_ready"); out_read = sem("out_read"); fin_relu = sem("fin_relu"); fin_ready = sem("fin_ready")

        def pad_rows(b, row, dy, dx, n):
            return pad[:, b, ds(row + dy, n), dx:dx + S]

        HATS = 9
        def hat_tile(par, i):
            return v8[:, par, :, :] if i == 8 else vt[:, par, i // 2, 2 * (i % 2):2 * (i % 2) + 2, :]
        HAT_STEP = (0, 1, 3, 4, 6, 7, 9, 10, 12)
        D_BANK, Y_BANK, Y8_BANK, O_BANK = (0, 1, 2), (3, 4), 5, (6, 7)
        ND = 3
        NORM_BANK = 7
        CONV_SPLIT = 2

        block = ctx.enter_context(nc.Block())

        @block.sync
        def _(sp):
            for q in range(Q):
                for b in range(2):
                    sp.dma_start(xv[C * q:C * q + C, b], x[2 * q + b]).then_inc(x_in, 16)
            sp.dma_start(wx_s, wx).then_inc(lstm_in, 16)
            sp.dma_start(whh_s, whh).then_inc(lstm_in, 16)
            sp.dma_start(wlin_s, wlin).then_inc(lstm_in, 16)
            sp.wait_ge(lin_ready, NCH)
            sp.dma_start(dmask, dm.bitcast(BF16)).then_inc(dmask_in, 16)
            sp.wait_ge(conv_ev, 2 + NCH)
            for a in range(2):
                sp.dma_start(ob[a][ONE_ROW + 1:ONE_ROW + 2, :], pos.bitcast(BF16)).then_inc(pos_in, 16)
            for c in range(8):
                sp.wait_ge(fin_ready, c + 1)
                b, h0 = c // 4, 16 * (c % 4)
                for q in range(Q):
                    sp.dma_start(out[2 * q + b, :, h0:h0 + 16, :],
                                 fin.rearrange("p (b h w) -> p b h w", b=2, h=S)[C * q:C * q + C, b, h0:h0 + 16]
                                 ).then_inc(stored, 16)
            sp.wait_ge(stored, 16 * 8 * Q)

        @block.gpsimd
        def _(pool):
            chain = [0]

            def step(ins):
                chain[0] += 1
                ins.then_inc(pool_chain, 1)
                pool.wait_ge(pool_chain, chain[0])

            nc.gpsimd.memset(y8[:, :, :, :, :], 0.0).then_inc(y8_zero, 1)
            nc.gpsimd.memset(gc, 0.0)
            nc.gpsimd.memset(seq[:, 0:SEQ], 0.0).then_inc(zeroed, 1)
            pool.wait_ge(o_ready, S)
            nc.gpsimd.memset(pad[:, :, 0:PAD:PAD - 1, :], 0.0).then_inc(pad_zero, 1)
            nc.gpsimd.memset(pad[:, :, 1:1 + S, 0:PAD:PAD - 1], 0.0).then_inc(pad_zero, 1)
            pool.wait_ge(part3, 2 + NCH)
            step(nc.gpsimd.memset(wm, 0.0))
            for a in range(2):
                for q in range(Q):
                    s_ = slice(C * q, C * q + C)
                    w3 = wc[s_, a, :].rearrange("p (k o) -> p k o", k=K)
                    nc.gpsimd.tensor_copy(wm[s_, a, q, 0:P].rearrange("p (k o) -> p k o", k=4), w3[:, 0:8:2, :])
                    nc.gpsimd.tensor_copy(wm[s_, a, q, P:2 * P].rearrange("p (k o) -> p k o", k=4), w3[:, 1:8:2, :])
                    last = nc.gpsimd.tensor_copy(wm[s_, a, q, 2 * P:2 * P + C], w3[:, 8, :])
            last.then_inc(wm_ready, 1)
            pool.wait_ge(wm_ready, 1)
            def chunk(a, b, r, g, fresh):
                for par in range(2):
                    if not fresh:
                        pool.wait_ge(y8_ready, r * 2 + (2 * g + par - 1))
                    r4 = ds(r * ROWS + (1 + HROWS * par), HROWS)
                    src = pad[:, b, r4, 1:1 + S] if a == 0 else pad[:, b, 1:1 + S, r4].rearrange("p h w -> p w h")
                    nc.gpsimd.tensor_copy(xc[:, par, :].rearrange("p (r n) -> p r n", r=HROWS), src).then_inc(xc_ready, 1)
            for a in range(2):
                for b in range(2):
                    g0 = a * NCH + b * 8
                    if g0 == 0:
                        chunk(a, b, 0, 0, True)
                    with pool.Fori(1 if g0 == 0 else 0, 8) as r:
                        chunk(a, b, r, g0, False)

        @block.scalar
        def _(act):
            act.dma_start(vecs[:, :], vec).then_inc(misc_in, 16)
            act.dma_start(avgs[:, :, :], avg).then_inc(misc_in, 16)
            act.dma_start(gb_f, gate_bias).then_inc(lstm_in, 16)
            act.dma_start(gi_b, gate_ind.bitcast(BF16)).then_inc(lstm_in, 16)
            act.dma_start(dsc_s, dsc).then_inc(conv_in, 16)
            act.dma_start(f23_s[:, 0:3, :], fus[1]).then_inc(conv_in, 16)
            act.dma_start(cw_s, cw).then_inc(conv_in, 16)
            act.dma_start(fus_s, fus[0]).then_inc(conv_in, 16)
            act.dma_start(pws[:, :, :], pw).then_inc(conv_in, 16)
            act.dma_start(sels[:, :, :], sel.bitcast(BF16)).then_inc(conv_in, 16)
            for a in range(2):
                act.wait_ge(fuse_mm, a + 1)
                nc.scalar.activation(wc[:, a, :], ps[a][:, 0:K * C], ACT.Copy, scale=-1.0).then_inc(fuse_ev, 1)
            act.wait_ge(fuse_mm, 3)
            for n in range(3):
                m = min(4, K - 4 * n) * P
                last = nc.scalar.activation(of[:, K * P + 4 * P * n:K * P + 4 * P * n + m], ps[2 + n][:, 0:m], ACT.Copy)
            nc.scalar.activation(cbias, ps[5][:, 0:1], ACT.Copy).then_inc(fuse_ev, 1)

            def norm_sqrt(i, n):
                act.wait_ge(sqrt_in, i + 1)
                nc.scalar.activation(nt[:, 3, 0:n], nt[:, 2, 0:n], ACT.Sqrt).then_inc(sqrt_out, 1)

            norm_sqrt(GN1, 2)
            def gates(s, par, wait):
                act.wait_ge(gif_ready, wait)
                nc.scalar.activation(sif, ps[2 * par][:, P:3 * P], ACT.Sigmoid)
                nc.scalar.activation(gc[:, 0:P], ps[2 * par][:, 0:P], ACT.Tanh).then_inc(sif_ready, 1)
                act.wait_ge(o_ready, wait)
                nc.scalar.activation(so, ps[2 * par + 1][:, 0:P], ACT.Sigmoid)
                act.wait_ge(c_ready, wait)
                nc.scalar.activation(tc_, gc[:, P:2 * P], ACT.Tanh).then_inc(tc_ready, 1)
            with act.Fori(0, S // 2) as it:
                for par in range(2):
                    gates(None, par, it * 2 + (par + 1))
            norm_sqrt(GN2, 2)
            nc.scalar.nop().then_inc(conv_ev, 2)
            with act.Fori(0, NCH // 2) as it:
                for par in range(2):
                    act.wait_ge(conv_mm, it * 2 + (par + 1))
                    nc.scalar.activation(acc[:, ds(it * (2 * CH) + par * CH, CH)], ps[par][:, :], ACT.Identity,
                                         bias=cbias[:, 0:1]).then_inc(conv_ev, 1)
            nc.scalar.nop().then_inc(part3, 2)
            for a in range(2):
                norm_sqrt(BNX + a, 1)
                act.wait_ge(norm_done, BNX + a + 1)
                for n in range(4):
                    v = wide[:, a * L + n * (L // 4):a * L + (n + 1) * (L // 4)]
                    nc.scalar.activation(v, v, ACT.Relu, bias=coef[:, BNX + a, 1, 0:1],
                                         scale=coef[:, BNX + a, 0, 0:1]).then_inc(relu_done, 1)
                with act.Fori(0, NCH // 4) as it:
                    for ready, done in ((off_mm, part1), (rest1, part2), (rest2, part3)):
                        for par in range(2):
                            act.wait_ge(ready, it * 2 + (a * NCH // 2 + par + 1))
                            act.sem_inc(act_turn, 1)
                            nc.scalar.activation(ob[a][0:ONE_ROW + 1, ds(it * (4 * CH) + par * 2 * CH, 2 * CH)],
                                                 psum[0:ONE_ROW + 1, par * 2 * CH:(par + 1) * 2 * CH], ACT.Identity,
                                                 bias=vecs[0:ONE_ROW + 1, V_PWB + a:V_PWB + a + 1]).then_inc(done, 1)
            with act.Fori(0, 2 * NCH) as g:
                for par in range(2):
                    for i in range(HATS):
                        act.wait_ge(d_ready, g * (2 * HATS) + (par * HATS + i + 1))
                        nc.scalar.activation(hat_tile(par, i), ps[D_BANK[i % ND]].rearrange("p (q n) -> p q n", q=2),
                                             ACT.Abs).then_inc(d_read, 1)
            norm_sqrt(BNF, 1)
            act.wait_ge(norm_done, BNF + 1)
            for c in range(8):
                v = ds(c * (L // 8), L // 8)
                nc.scalar.activation(fin[:, v], acc[:, v], ACT.Relu, bias=coef[:, BNF, 1, 0:1],
                                     scale=coef[:, BNF, 0, 0:1]).then_inc(fin_relu, 1)

        @block.vector
        def _(dve):
            chain = [0]

            def step(ins):
                chain[0] += 1
                ins.then_inc(link, 1)
                dve.wait_ge(link, chain[0])

            def norm(i, n, eps, gamma, beta):
                v = nc.vector
                m, var = mv[:, 0:n, 0], mv[:, 0:n, 1]
                t = [nt[:, j, 0:n] for j in range(8)]
                sc, sh = coef[:, i, 0, 0:n], coef[:, i, 1, 0:n]
                gm, gv = ps[NORM_BANK][:, 0:n], ps[NORM_BANK][:, 8:8 + n]
                v.tensor_copy(t[0], m).then_inc(mean_in, 1)
                dve.wait_ge(mean_out, i + 1)
                step(v.tensor_copy(t[6], gm))
                step(v.tensor_tensor(t[1], m, t[6], ALU.subtract))
                step(v.tensor_tensor(t[1], t[1], t[1], ALU.mult))
                v.tensor_tensor(t[1], t[1], var, ALU.add).then_inc(dev_in, 1)
                dve.wait_ge(var_out, i + 1)
                v.tensor_scalar(t[2], gv, float(eps), None, ALU.add).then_inc(sqrt_in, 1)
                dve.wait_ge(sqrt_out, i + 1)
                step(v.reciprocal(t[4], t[3]))
                step(v.tensor_tensor(t[5], t[4], t[4], ALU.mult))
                step(v.tensor_tensor(t[5], t[5], t[2], ALU.mult))
                step(v.tensor_scalar(t[5], t[5], -0.5, 1.5, ALU.mult, ALU.add))
                step(v.tensor_tensor(sc, t[4], t[5], ALU.mult))
                if gamma is not None:
                    step(v.tensor_tensor(sc, sc, gamma, ALU.mult))
                step(v.tensor_tensor(t[7], t[6], sc, ALU.mult))
                if beta is None:
                    ins = v.tensor_scalar(sh, t[7], -1.0, None, ALU.mult)
                else:
                    ins = v.tensor_tensor(sh, beta, t[7], ALU.subtract)
                ins.then_inc(norm_done, 1)
                dve.wait_ge(norm_done, i + 1)

            def stats_of(src, b):
                for r in range(NCH // 2):
                    n = b * (NCH // 2) + r
                    last = nc.vector.bn_stats(stats[:, n, :], src(b, r))
                return last

            def aggregate(n):
                for j in range(n):
                    k = NCH // n
                    last = nc.vector.bn_aggr(mv[:, j, :], stats[:, j * k:(j + 1) * k, :])
                step(last)

            flat = lambda t: (lambda b, r: t[:, b * PIX + r * CH:b * PIX + (r + 1) * CH])

            dve.wait_ge(x_in, 16 * 2 * Q)
            stats_of(flat(xs), 0)
            step(stats_of(flat(xs), 1))
            aggregate(2)
            dve.wait_ge(misc_in, 32)
            norm(GN1, 2, GN_EPS, None, None)
            for b in range(2):
                nc.vector.tensor_scalar(xg[:, b], xv[:, b], coef[:, GN1, 0, b:b + 1], coef[:, GN1, 1, b:b + 1],
                                        ALU.mult, ALU.add).then_inc(xg_ready, 1)
            dve.wait_ge(lstm_in, 16 * 5)
            step(nc.vector.tensor_tensor(gb_r, gb_f[:, 0, :], gb_f[:, 1, :], ALU.add))
            step(nc.vector.tensor_copy(gb_1, gb_r))
            step(nc.vector.scalar_tensor_tensor(gb_r, gb_1, vecs[0:12, V_G1:V_G1 + 1], gb_r, ALU.mult, ALU.add))
            step(nc.vector.tensor_copy(gb_2, gb_r))
            nc.vector.scalar_tensor_tensor(gb_b, gb_2, vecs[0:12, V_G2:V_G2 + 1], gb_r,
                                           ALU.mult, ALU.add).then_inc(gb_ready, 1)
            dve.wait_ge(zeroed, 1)
            nc.vector.nop().then_inc(h_ready, 1)
            with dve.Fori(0, S) as s_:
                dve.wait_ge(sif_ready, s_ + 1)
                nc.vector.tensor_tensor(prod, sif, gc, ALU.mult).then_inc(prod_ready, 1)
                dve.wait_ge(prod_ready, s_ + 1)
                nc.vector.tensor_tensor(gc[:, P:2 * P], prod[:, 0:P], prod[:, P:2 * P], ALU.add).then_inc(c_ready, 1)
                dve.wait_ge(tc_ready, s_ + 1)
                nc.vector.tensor_tensor(seq[:, ds((s_ + 1) * SEQ, SEQ)], so, tc_, ALU.mult).then_inc(h_ready, 1)
            nc.vector.nop().then_inc(x1_ready, 4)
            with dve.Fori(0, NCH // 2) as it:
                for par in range(2):
                    dve.wait_ge(lin_ready, it * 2 + (par + 1))
                    for b in range(2):
                        xr = xv[:, b, ds(it * 8 + 4 * par, 4), :]
                        nc.vector.scalar_tensor_tensor(
                            xr, ps[4 + par][:, :].rearrange("p (f b t) -> p b f t", f=4, b=2)[:, b],
                            vecs[:, V_BLIN:V_BLIN + 1], xr, ALU.add, ALU.add).then_inc(x1_ready, 1)
            dve.wait_ge(x1_ready, 4 + 2 * NCH)
            stats_of(flat(xs), 0)
            step(stats_of(flat(xs), 1))
            aggregate(2)
            norm(GN2, 2, GN_EPS, None, None)
            dve.wait_ge(pad_zero, 2)
            for b in range(2):
                nc.vector.tensor_scalar(pad[:, b, 1:1 + S, 1:1 + S], xv[:, b], coef[:, GN2, 0, b:b + 1],
                                        coef[:, GN2, 1, b:b + 1], ALU.mult, ALU.add).then_inc(pad_ready, 1)
            dve.wait_ge(pad_ready, 2)
            for a in range(2):
                for t in range(9):
                    for b in range(2):
                        src = pad_rows(b, 0, t // 3, t % 3, S)
                        w = vecs[:, V_DW + 9 * a + t:V_DW + 9 * a + t + 1]
                        if t == 0:
                            ins = nc.vector.tensor_scalar(hv[a][:, b], src, w, vecs[:, V_DWB + a:V_DWB + a + 1],
                                                          ALU.mult, ALU.add)
                        else:
                            dve.wait_ge(dw_done, 18 * a + 2 * t + b - 1)
                            ins = nc.vector.scalar_tensor_tensor(hv[a][:, b], src, w, hv[a][:, b], ALU.mult, ALU.add)
                        ins.then_inc(dw_done, 1)
                dve.wait_ge(dw_done, 18 * (a + 1))
                h = (h_x, h_y)[a]
                stats_of(flat(h), 0)
                step(stats_of(flat(h), 1))
                aggregate(1)
                norm(BNX + a, 1, BN_EPS, vecs[:, V_BNG + a:V_BNG + a + 1], vecs[:, V_BNB + a:V_BNB + a + 1])
            nc.vector.nop().then_inc(out_read, 2)
            dve.wait_ge(y8_zero, 1)

            def hats(r, g, par):
                for i in range(HATS):
                    v = hat_tile(par, i)
                    dve.wait_ge(d_read, r * (2 * HATS) + (g * 2 * HATS + par * HATS + i + 1))
                    nc.vector.tensor_scalar(v, v, 1.0, 1.0, ALU.min, ALU.subtract).then_inc(v_ready, 1)
                    if i % 2 == 1 and i > 1:
                        evac_y(r, g, par, i // 2 - 1)
                evac_y(r, g, par, 3)
                dve.wait_ge(y8_ready, r * 2 + (2 * g + par + 1))
                for e in range(2):
                    last = nc.vector.tensor_copy(
                        y8[S * e:S * e + S, par, e:Q:2, :, :],
                        ps[Y8_BANK][S * e:S * e + S, 0:2 * HROWS * C].rearrange("p (q r m) -> p q r m", q=2, r=HROWS))
                last.then_inc(y8_read, 1)

            def evac_y(r, g, par, q):
                dve.wait_ge(y_ready, r * (2 * Q) + (g * 2 * Q + par * Q + q + 1))
                nc.vector.tensor_copy(yt[:, par, q, :, :], ps[Y_BANK[q % 2]].rearrange("p (r m) -> p r m", r=HROWS)
                                      ).then_inc(y_read, 1)

            def gather(a, b, r, par, count):
                r4 = ds(r * ROWS + HROWS * par, HROWS)
                v = accv[:, b, r4, :] if a == 0 else accv[:, b, :, r4].rearrange("p h w -> p w h")
                dve.wait_ge(out_ready, count)
                nc.vector.tensor_tensor(v, ps[O_BANK[par]][:, 0:SL].rearrange("p (r n) -> p r n", r=HROWS), v,
                                        ALU.add).then_inc(out_read, 1)

            dve.wait_ge(part3, 2 + NCH)
            for a in range(2):
                for b in range(2):
                    g0 = a * NCH + b * 8
                    def chunk(r, rprev, ahead):
                        hats(r, g0, 0)
                        if ahead:
                            gather(a, b, rprev, 1, r * 2 + 2 * g0)
                        elif g0:
                            gather((g0 // 8 - 1) // 2, (g0 // 8 - 1) % 2, 7, 1, 2 * g0)
                        hats(r, g0, 1)
                        gather(a, b, r, 0, r * 2 + (2 * g0 + 1))
                    chunk(0, None, False)
                    with dve.Fori(1, 8) as r:
                        chunk(r, r - 1, True)
            gather(1, 1, 7, 1, 2 * 2 * NCH)
            dve.wait_ge(out_read, 2 + 2 * 2 * NCH)
            stats_of(flat(acc), 0)
            step(stats_of(flat(acc), 1))
            aggregate(1)
            norm(BNF, 1, BN_EPS, vecs[:, V_FG:V_FG + 1], vecs[:, V_FB:V_FB + 1])
            for c in range(8):
                v = ds(c * (L // 8), L // 8)
                dve.wait_ge(fin_relu, c + 1)
                nc.vector.tensor_tensor(fin[:, v], fin[:, v], xs[:, v], ALU.add).then_inc(fin_ready, 1)

        @block.tensor
        def _(pe):
            mm = nc.tensor.matmul

            def norm_mm(i, n):
                m = avgs[:, 0 if i <= GN2 else 1, :]
                pe.wait_ge(mean_in, i + 1)
                mm(ps[NORM_BANK][:, 0:n], m, nt[:, 0, 0:n], start=True, stop=True).then_inc(mean_out, 1)
                pe.wait_ge(dev_in, i + 1)
                mm(ps[NORM_BANK][:, 8:8 + n], m, nt[:, 1, 0:n], start=True, stop=True).then_inc(var_out, 1)

            pe.wait_ge(conv_in, 16 * 6)
            for a in range(2):
                for k in range(K):
                    last = mm(ps[a][:, k * C:(k + 1) * C], dsc_s[:, a, k, :], f23_s[:, a, :], start=(k == 0), stop=(k == K - 1))
                last.then_inc(fuse_mm, 1)
            for t in range(9):
                last = mm(ps[2 + t // 4][:, (t % 4) * P:(t % 4 + 1) * P], cw_s[:, t, :], fus_s, start=(t % 4 == 0), stop=(t % 4 == 3 or t == 8))
            pe.wait_ge(misc_in, 32)
            mm(ps[5][:, 0:1], fus_s, vecs[:, V_CONVB:V_CONVB + 1], start=True, stop=True).then_inc(fuse_mm, 1)
            norm_mm(GN1, 2)

            def gates_x(f, fb, par):
                mm(ps[2 * par][:, 0:3 * P], gb_b, gi_b[:, 0:3 * P], start=True, stop=False)
                mm(ps[2 * par + 1][:, 0:P], gb_b, gi_b[:, 3 * P:4 * P], start=True, stop=False)
                for g in range(4):
                    for d, row in enumerate((f, fb)):
                        mm(ps[2 * par + g // 3][:, (g % 3) * P:(g % 3 + 1) * P], wx_s[:, d, g, :], xg[:, :, row, :],
                           start=False, stop=False)

            def gates_h(col, par, count):
                pe.wait_ge(h_ready, count)
                for g in range(4):
                    last = mm(ps[2 * par + g // 3][:, (g % 3) * P:(g % 3 + 1) * P], whh_s[:, g, :], seq[:, col],
                              start=False, stop=(g >= 2))
                    if g == 2:
                        last.then_inc(gif_ready, 1)
                last.then_inc(o_ready, 1)

            pe.wait_ge(lstm_in, 16 * 5)
            pe.wait_ge(gb_ready, 1)
            pe.wait_ge(xg_ready, 2)
            pe.wait_ge(fuse_ev, 3)
            gates_x(0, S - 1, 0)
            with pe.Fori(0, S // 2 - 1) as it:
                for par in range(2):
                    gates_h(ds(it * (2 * SEQ) + par * SEQ, SEQ), par, it * 2 + (par + 1))
                    gates_x(ds(it * 2 + (par + 1), 1), ds(it * -2 + (S - 2 - par), 1), 1 - par)
            gates_h(ds((S - 2) * SEQ, SEQ), 0, S - 1)
            gates_x(S - 1, 0, 1)
            gates_h(ds((S - 1) * SEQ, SEQ), 1, S)
            pe.wait_ge(h_ready, S + 1)
            with pe.Fori(0, NCH // 2) as it:
                for par in range(2):
                    pe.wait_ge(x1_ready, it * 4 + (2 * par + 2))
                    mm(ps[4 + par][:, :], wlin_s[:, 0, :], seq[:, ds(it * (8 * SEQ) + (4 * par + 1) * SEQ, 4 * SEQ)],
                       start=True, stop=False)
                    for i in range(4):
                        last = mm(ps[4 + par][:, i * SEQ:(i + 1) * SEQ], wlin_s[:, 1, :],
                                  seq[:, ds(it * (-8 * SEQ) + (S - 4 * par - i) * SEQ, SEQ)], start=False, stop=(i == 3))
                    last.then_inc(lin_ready, 1)
            norm_mm(GN2, 2)
            pe.wait_ge(pad_ready, 2)
            def conv(b, lo, hi):
                with pe.Fori(lo, hi) as it:
                    for par in range(2):
                        pe.wait_ge(conv_ev, it * 2 + (8 * b + par + 1))
                        for t in range(9):
                            last = mm(ps[par], cwf[:, t, :], pad_rows(b, it * (2 * ROWS) + ROWS * par, t // 3, t % 3, ROWS),
                                      start=(t == 0), stop=(t == 8))
                        last.then_inc(conv_mm, 1)
            conv(0, 0, 4)
            conv(1, 0, CONV_SPLIT)
            norm_mm(BNX, 1)
            conv(1, CONV_SPLIT, 4)
            pe.wait_ge(conv_ev, 2 + NCH)
            pe.wait_ge(dmask_in, 16)
            for a in range(2):
                if a == 1:
                    norm_mm(BNY, 1)
                pe.wait_ge(relu_done, 4 * (a + 1))
                for b in range(2):
                    with pe.Fori(0, 2) as it:
                        for n in range(4):
                            if n % 2 == 0:
                                pe.wait_ge(part3, it * 2 + (a * NCH // 2 + 4 * b + n // 2 + 1))
                            r0 = ds(it * (4 * ROWS) + ROWS * n, ROWS)
                            rhs = hv[a][:, b, r0, :] if a == 0 else hv[a][:, b, :, r0].rearrange("p h w -> p w h")
                            last = mm(ps[n][0:NROW, :], pws[:, a, :], rhs, start=True, stop=True)
                            if n % 2 == 1:
                                last.then_inc(off_mm, 1)
                        for m, (ready, done) in enumerate(((part1, rest1), (part2, rest2))):
                            for n in range(4):
                                if n % 2 == 0:
                                    pe.wait_ge(ready, it * 2 + (a * NCH // 2 + 4 * b + n // 2 + 1))
                                last = mm(ps[n][0:NROW, :], dmask[:, m, :],
                                          ob[a][0:ONE_ROW + 1, ds(it * (4 * CH) + (8 * b + n) * CH, CH)],
                                          start=False, stop=True, skip_group_check=True)
                                if n % 2 == 1:
                                    last.then_inc(done, 1)
            def dist(s, slots, par, off, i):
                if not (isinstance(s, int) and (s + slots) * HATS + i < ND):
                    pe.wait_ge(d_read, s * HATS + (slots * HATS + i - ND + 1))
                for e in range(2):
                    k = 4 * Q + e if i == 8 else 4 * (2 * (i % 2) + e) + i // 2
                    last = mm(ps[D_BANK[i % ND]][:, e * SL:(e + 1) * SL], sels[:, k, :], offs[0:NROW, off],
                              start=(e == 0), stop=(e == 1))
                last.then_inc(d_ready, 1)

            def project(a, s, slots, par, q, r):
                x_r = xc[:, par, r * S:(r + 1) * S]
                if r == 0 and not (isinstance(s, int) and (s + slots) * Q + q < 2):
                    pe.wait_ge(y_read, s * Q + (slots * Q + q - 1))
                for e in range(2):
                    last = mm(ps[Y_BANK[q % 2]][S * e:S * e + S, r * P:(r + 1) * P], x_r, wm[:, a, q, e * P:(e + 1) * P],
                              start=(r == 0), stop=(r == HROWS - 1))
                if r == HROWS - 1:
                    last.then_inc(y_ready, 1)
                if q == 0 and r == 0 and not (isinstance(s, int) and s + slots < 1):
                    pe.wait_ge(y8_read, s + slots)
                e, n = q % 2, (q // 2) * HROWS + r
                last = mm(ps[Y8_BANK][S * e:S * e + S, n * C:(n + 1) * C], x_r, wm[:, a, q, 2 * P:2 * P + C],
                          start=(n == 0), stop=(n == 2 * HROWS - 1))
                if q == Q - 1 and r == HROWS - 1:
                    last.then_inc(y8_ready, 1)

            GROUPS = HROWS * 5
            STEPS = Q * HROWS
            LEAD = 4

            def product(par, group):
                r, k = group // 5, group % 5
                cols = slice(r * S, (r + 1) * S)
                for q in range(Q):
                    w, v = ((y8[:, par, q, r, :], v8[:, par, q // 2, cols]) if k == 4 else
                            (yt[:, par, q, r, k * C:(k + 1) * C], vt[:, par, k, q, cols]))
                    last = mm(ps[O_BANK[par]][C * q:C * q + C, cols], w, v, start=(group == 0), stop=(group == GROUPS - 1))
                if group == GROUPS - 1:
                    last.then_inc(out_ready, 1)

            def slot(a, s, slots, par, off):
                for i in range(STEPS):
                    if off is not None:
                        nslots = 0 if slots is None else slots + 1
                        if i == 0:
                            pe.wait_ge(xc_ready, s + (nslots + 1))
                        if i in HAT_STEP:
                            dist(s, nslots, 1 - par, off, HAT_STEP.index(i))
                        project(a, s, nslots, 1 - par, i // HROWS, i % HROWS)
                    if slots is not None and i >= LEAD:
                        if i == LEAD:
                            pe.wait_ge(v_ready, s * HATS + (slots + 1) * HATS)
                            pe.wait_ge(y_read, s * Q + (slots + 1) * Q)
                            pe.wait_ge(y8_read, s + (slots + 1))
                            pe.wait_ge(out_read, s + (slots + 1))
                        j, n = i - LEAD, STEPS - LEAD
                        for group in range(j * GROUPS // n, (j + 1) * GROUPS // n):
                            product(par, group)

            pe.wait_ge(pos_in, 32)
            pe.wait_ge(part3, 2 + NCH)
            pe.wait_ge(wm_ready, 1)
            for a in range(2):
                s0 = 2 * a * NCH
                slot(a, s0, None, 1, ds(a * L, SL))
                with pe.Fori(0, NCH - 1) as g:
                    for par in range(2):
                        slot(a, g * 2, s0 + par, par, ds(g * CH + (a * L + (par + 1) * SL), SL))
                slot(a, 2 * NCH - 2, s0, 0, ds(a * L + L - SL, SL))
                slot(a, 2 * NCH - 2, s0 + 1, 1, None)
            norm_mm(BNF, 1)


def layout(inputs):
    import numpy as np
    f = np.float32
    g = {k: np.asarray(v) for k, v in inputs.items()}
    order = (2, 0, 1, 3)
    wx = np.zeros((P, 2, 4, P), f)
    whh = np.zeros((P, 4, P), f)
    wlin = np.zeros((P, 2, P), f)
    gb = np.zeros((12, 2, P), f)
    for q in range(Q):
        for d, n in enumerate("fb"):
            col = slice(q * 32 + d * HID, q * 32 + (d + 1) * HID)
            wih, wh = g[f"L0_conv_W_ih_{n}"], g[f"L0_conv_W_hh_{n}"]
            for j, t in enumerate(order):
                wx[q * 32:(q + 1) * 32, d, j, col] = wih[t * HID:(t + 1) * HID].T
                whh[col, j, col] = wh[t * HID:(t + 1) * HID].T
                for p in range(PARTS):
                    gb[4 * p + j, 0, col] = g[f"L0_conv_b_ih_{n}"][t * HID:(t + 1) * HID]
                    gb[4 * p + j, 1, col] = g[f"L0_conv_b_hh_{n}"][t * HID:(t + 1) * HID]
            wlin[col, d, q * 32:(q + 1) * 32] = g["L0_conv_W_lin"][:, d * HID:(d + 1) * HID].T
    gi = np.zeros((12, CH), f)
    for p in range(PARTS):
        for j in range(4):
            gi[4 * p + j, j * P:(j + 1) * P] = 1
    cw = np.zeros((P, K, P), f)
    fus = np.zeros((P, P), f)
    fw = g["L1_conv_fus_w"][:, :, 0, 0]
    for q in range(Q):
        s = slice(q * 32, (q + 1) * 32)
        for t in range(9):
            cw[s, t, s] = g["L1_conv_conv_w"][:, :, t // 3, t % 3]
        fus[s, s] = fw[:, 0:32].T
    f23 = np.zeros((C, 3, C), f)
    f23[:, 0] = fw[:, 32:64].T
    f23[:, 1] = fw[:, 64:96].T
    dsc = np.zeros((C, 2, K, P), f)
    pw = np.zeros((P, 2, NROW), f)
    vec = np.zeros((P, NVEC), f)
    for a, n in enumerate("xy"):
        w = g[f"L1_conv_dsc{n}_w"]
        pww, pwb = g[f"L1_conv_off{n}_pw_w"][:, :, 0, 0], g[f"L1_conv_off{n}_pw_b"]
        for q in range(Q):
            s = slice(q * 32, (q + 1) * 32)
            for k in range(K):
                dsc[:, a, k, s] = w[:, :, k]
            for p in range(PARTS):
                r = p * NOFF + q * K
                pw[s, a, r:r + K] = pww.T
                vec[r:r + K, V_PWB + a] = pwb
            vec[s, V_DWB + a] = g[f"L1_conv_off{n}_dw_b"]
            vec[s, V_BNG + a] = g[f"L1_conv_off{n}_bn_g"]
            vec[s, V_BNB + a] = g[f"L1_conv_off{n}_bn_b"]
            vec[s, V_DW + 9 * a:V_DW + 9 * a + 9] = g[f"L1_conv_off{n}_dw_w"].reshape(C, 9)
        vec[ONE_ROW, V_PWB + a] = 1
    for q in range(Q):
        s = slice(q * 32, (q + 1) * 32)
        vec[s, V_BLIN] = g["L0_conv_b_lin"]
        vec[s, V_CONVB] = g["L1_conv_conv_b"]
        vec[s, V_FG] = g["L1_conv_fus_bn_g"]
        vec[s, V_FB] = g["L1_conv_fus_bn_b"]
    vec[4:12, V_G1] = -1
    vec[8:12, V_G2] = -1
    ch = np.arange(P)
    avg = np.zeros((P, 2, P), f)
    avg[:, 0] = 0.5 * (ch[:, None] // 2 == ch[None] // 2)
    avg[:, 1] = 0.25 * (ch[:, None] % C == ch[None] % C)
    sel = np.zeros((NROW, NSEL, P), f)
    for n in range(NSEL):
        for e in range(2):
            q, k = (n // 4, 2 * (n % 4) + e) if n < 4 * Q else (2 * (n - 4 * Q) + e, 8)
            for p in range(PARTS):
                sel[p * NOFF + q * K + k, n, e * S:(e + 1) * S] = 1
            sel[ONE_ROW, n, e * S:(e + 1) * S] = -np.arange(S)
            sel[ONE_ROW + 1, n, e * S:(e + 1) * S] = 1
    dm = np.zeros((ONE_ROW + 1, 2, NROW), f)
    for m in range(2):
        rows = np.arange((m + 1) * NOFF, ONE_ROW)
        dm[rows, m, rows] = -1
    pos = np.tile(np.arange(S), L // S)[None].astype(f)
    bits = lambda a: (a.view(np.uint32) >> 16).astype(np.uint16)
    return dict(x=g["x"], wx=wx, whh=whh, wlin=wlin, gate_bias=gb, gate_ind=bits(gi), cw=cw, fus=fus, f23=f23,
                dsc=dsc, pw=pw, dm=bits(dm), vec=vec, avg=avg, sel=bits(sel), pos=bits(pos))


def kernel(**inputs):
    import numpy as _np
    import concourse.bacc as _bacc
    from concourse import mybir as _mybir
    from concourse.bass_utils import run_bass_kernel_spmd as _run

    nc = _bacc.Bacc("TRN2", target_bir_lowering=False, num_devices=1)
    arrays, args = {}, {}
    for name, a in layout(inputs).items():
        a = _np.ascontiguousarray(a)
        arrays[f"in_{name}_dram"] = a
        args[name] = nc.dram_tensor(f"in_{name}_dram", a.shape, _mybir.dt.from_np(a.dtype), kind="ExternalInput").ap()
    args["fus"] = (args["fus"], args.pop("f23"))
    out = nc.dram_tensor("out_0_dram", (2 * Q, C, S, S), _mybir.dt.float32, kind="ExternalOutput").ap()
    build(nc, out=out, **args)
    r = _run(nc, [arrays], core_ids=[0])
    return r.results[0]["out_0_dram"]
```

```python
import concourse.bass as bass
from concourse import mybir
from contextlib import ExitStack

F32 = mybir.dt.float32
BF16 = mybir.dt.bfloat16
P = 128
Q = 4
C = 32
S = 64
PIX = S * S
L = 2 * PIX
HID = 16
K = 9
SEQ = 2 * S
DQ = Q * HID
GROUP = 4
NG = S // GROUP
ROWS = 8
CH = ROWS * S
NCH = L // CH
PAD = S + 2
PARTS = 3
NOFF = Q * K
ONE_ROW = PARTS * NOFF
NROW = ONE_ROW + 2
HROWS = ROWS // 2
SL = HROWS * S
NSEL = Q * 4 + 2
GN_EPS = 1e-5
BN_EPS = 1e-5
GN1, GN2, BNX, BNY, BNF = range(5)

(V_BLIN, V_CONVB, V_FG, V_FB, V_G1, V_G2) = range(6)
V_DWB, V_BNG, V_BNB, V_PWB = 6, 8, 10, 12
V_DW = 14
NVEC = V_DW + 18


def build(nc, x, wx, whh, wlin, gate_bias, gate_ind, cw, fus, dsc, pw, dm, vec, avg, sel, pos, out):
    ACT = mybir.ActivationFunctionType
    ALU = mybir.AluOpType
    AX = mybir.AxisListType
    ds = bass.ds
    ctx = ExitStack()
    with ctx:
        def sb(name, shape, dt=F32):
            return ctx.enter_context(nc.sbuf_tensor(name, shape, dt))

        def sem(name):
            return ctx.enter_context(nc.semaphore(name))

        xs = sb("xs", [P, L])
        img = sb("img", [P, 2 * PAD * PAD])
        seq = sb("seq", [P, L + P])
        wide = sb("wide", [P, 2 * L])
        offs = sb("offs", [P, 2 * L], BF16)
        wc = sb("wc", [P, 2, K * C])
        vecs = sb("vecs", [P, NVEC])
        avgs = sb("avgs", [P, 2, P])
        sels = sb("sels", [NROW, NSEL, P], BF16)
        pws = sb("pws", [P, 2, NROW])
        y8 = sb("y8", [P, 2, Q, HROWS, C])
        stats = sb("stats", [P, NCH, 6])
        small = sb("small", [P, 41])
        mv = small[:, 0:4].rearrange("p (n a) -> p n a", a=2)
        nt = small[:, 4:20].rearrange("p (a n) -> p a n", n=2)
        coef = small[:, 20:40].rearrange("p (i a n) -> p i a n", a=2, n=2)
        cbias = small[:, 40:41]
        psum = ctx.enter_context(nc.psum_tensor("psum", [P, 8 * CH], F32))
        ps = [psum[:, i * CH:(i + 1) * CH] for i in range(8)]

        xv = xs[:, :].rearrange("p (b f t) -> p b f t", b=2, f=S)
        xg = img[:, 0:L].rearrange("p (b f t) -> p b f t", b=2, f=S)
        pad = img[:, :].rearrange("p (b h w) -> p b h w", b=2, h=PAD)
        acc = seq[:, 0:L]
        hall = seq[:, 0:L].rearrange("p (f b t) -> p f b t", f=S, b=2)
        accv = acc.rearrange("p (b h w) -> p b h w", b=2, h=S)

        o = 0
        def region(n):
            nonlocal o
            o += n
            return wide[:, o - n:o]
        wx_s = region(2 * 4 * DQ).rearrange("p (d g m) -> p d g m", d=2, g=4)
        whh_s = region(4 * P).rearrange("p (g m) -> p g m", g=4)
        wlin_s = region(P)
        gb_f = region(2 * P)[0:12, :].rearrange("p (a m) -> p a m", a=2)
        gb_r = region(P)[0:12, :]
        gb_1 = region(P // 2)[0:12, :].bitcast(BF16)
        gb_2 = region(P // 2)[0:12, :].bitcast(BF16)
        gb_b = region(P // 2)[0:12, :].bitcast(BF16)
        gi_b = region(2 * GROUP * S)[0:12, :].bitcast(BF16)
        gc = region(2 * 2 * S).rearrange("p (b n) -> p b n", b=2)
        sifo = region(2 * 3 * S).rearrange("p (b n) -> p b n", b=2)
        prod = region(2 * 2 * S).rearrange("p (b n) -> p b n", b=2)
        tc_ = region(2 * S).rearrange("p (b n) -> p b n", b=2)
        hst = region(2 * GROUP * SEQ).rearrange("p (s n) -> p s n", s=2 * GROUP)
        xst = region(2 * 2 * GROUP * SEQ).rearrange("p (s d f n) -> p s d f n", s=2, d=2, f=GROUP)
        dsc_s = region(2 * K * P)[0:C, :].rearrange("p (a k m) -> p a k m", a=2, k=K)
        f23_s = region(3 * C)[0:C, :].rearrange("p (a m) -> p a m", a=3)
        assert o <= 2 * L
        h_x = wide[:, 0:L]
        h_y = wide[:, L:2 * L]
        hxv = h_x.rearrange("p (b h w) -> p b h w", b=2, h=S)
        hyv = h_y.rearrange("p (b h w) -> p b h w", b=2, h=S)
        hv = (hxv, hyv)

        o = 0
        vt = region(2 * 4 * Q * SL).rearrange("p (a k q n) -> p a k q n", a=2, k=4, q=Q)
        v8 = region(2 * 2 * SL).rearrange("p (a q n) -> p a q n", a=2, q=2)
        yt = region(2 * Q * HROWS * P).rearrange("p (a q r m) -> p a q r m", a=2, q=Q, r=HROWS)
        xc = region(2 * SL).rearrange("p (a n) -> p a n", a=2)
        wm = region(2 * Q * K * C).rearrange("p (a q n) -> p a q n", a=2, q=Q)
        assert o <= 2 * L
        fin = h_y

        of = offs[:, :].bitcast(F32)
        cw_s = of[:, 0:K * P].rearrange("p (k m) -> p k m", k=K)
        cwf = of[:, K * P:2 * K * P].rearrange("p (k m) -> p k m", k=K)
        fus_s = of[:, 2 * K * P:2 * K * P + P]
        dmask = seq[0:ONE_ROW + 1, L:L + NROW].bitcast(BF16).rearrange("p (a n) -> p a n", a=2)
        ob = [offs[:, a * L:(a + 1) * L] for a in range(2)]

        x_in = sem("x_in"); lstm_in = sem("lstm_in"); conv_in = sem("conv_in"); misc_in = sem("misc_in")
        pos_in = sem("pos_in"); dmask_in = sem("dmask_in"); act_turn = sem("act_turn"); stored = sem("stored")
        mean_in = sem("mean_in"); mean_out = sem("mean_out"); dev_in = sem("dev_in")
        var_out = sem("var_out"); sqrt_in = sem("sqrt_in"); sqrt_out = sem("sqrt_out")
        norm_done = sem("norm_done"); link = sem("link")
        xg_ready = sem("xg_ready"); gb_ready = sem("gb_ready")
        gates_ready = [sem(f"gates_ready{b}") for b in range(2)]
        sig_ready = [sem(f"sig_ready{b}") for b in range(2)]
        prod_ready = [sem(f"prod_ready{b}") for b in range(2)]
        c_ready = [sem(f"c_ready{b}") for b in range(2)]
        tc_ready = [sem(f"tc_ready{b}") for b in range(2)]
        h_ready = [sem(f"h_ready{b}") for b in range(2)]
        xst_ready = sem("xst_ready"); x_used = sem("x_used"); h_stored = sem("h_stored"); hf_stored = sem("hf_stored"); pool_turn = sem("pool_turn")
        pe_turn = sem("pe_turn")
        lin_ready = sem("lin_ready"); x1_ready = sem("x1_ready")
        fuse_mm = sem("fuse_mm"); zeroed = sem("zeroed"); fuse_ev = sem("fuse_ev"); pool_chain = sem("pool_chain")
        pad_zero = sem("pad_zero"); pad_ready = sem("pad_ready");
        conv_mm = sem("conv_mm"); conv_ev = sem("conv_ev")
        dw_done = sem("dw_done"); relu_done = sem("relu_done")
        off_mm = sem("off_mm"); part1 = sem("part1"); rest1 = sem("rest1")
        part2 = sem("part2"); rest2 = sem("rest2"); part3 = sem("part3"); rows_set = sem("rows_set")
        wm_zero = sem("wm_zero"); wm_ready = sem("wm_ready"); y8_zero = sem("y8_zero")
        xc_ready = sem("xc_ready"); d_ready = sem("d_ready"); d_read = sem("d_read"); v_ready = sem("v_ready")
        y_ready = sem("y_ready"); y_read = sem("y_read"); y8_ready = sem("y8_ready"); y8_read = sem("y8_read")
        out_ready = sem("out_ready"); out_read = sem("out_read"); fin_relu = sem("fin_relu"); fin_ready = sem("fin_ready")

        def pad_rows(b, row, dy, dx, n):
            return pad[:, b, ds(row + dy, n), dx:dx + S]

        def stream_gates(b, j):
            c0 = (4 * (j // GROUP) + 2 * b) * CH
            return psum[:, c0:c0 + 2 * CH].rearrange("p (g f t) -> p g f t", g=4, f=GROUP)[:, :, j % GROUP]

        UNROLL = 2 * GROUP

        ACT_UNROLL = 2 * UNROLL

        HATS = 9
        def hat_tile(par, i):
            return v8[:, par, :, :] if i == 8 else vt[:, par, i // 2, 2 * (i % 2):2 * (i % 2) + 2, :]
        HAT_STEP = (0, 1, 3, 4, 6, 7, 9, 10, 12)
        D_BANK, Y_BANK, Y8_BANK, O_BANK = (0, 1, 2), (3, 4), 5, (6, 7)
        ND = 3
        NORM_BANK = 7
        CONV_SPLIT = 2

        block = ctx.enter_context(nc.Block())

        @block.sync
        def _(sp):
            for q in range(Q):
                for b in range(2):
                    sp.dma_start(xv[C * q:C * q + C, b], x[2 * q + b]).then_inc(x_in, 16)
            sp.dma_start(wx_s, wx).then_inc(lstm_in, 16)
            sp.dma_start(whh_s, whh).then_inc(lstm_in, 16)
            sp.dma_start(wlin_s, wlin).then_inc(lstm_in, 16)
            sp.wait_ge(lin_ready, NCH)
            sp.dma_start(dmask, dm.bitcast(BF16)).then_inc(dmask_in, 16)
            sp.wait_ge(conv_ev, 2 + NCH)
            for a in range(2):
                sp.dma_start(ob[a][ONE_ROW + 1:ONE_ROW + 2, :], pos.bitcast(BF16)).then_inc(pos_in, 16)
            for c in range(8):
                sp.wait_ge(fin_ready, c + 1)
                b, h0 = c // 4, 16 * (c % 4)
                for q in range(Q):
                    sp.dma_start(out[2 * q + b, :, h0:h0 + 16, :],
                                 fin.rearrange("p (b h w) -> p b h w", b=2, h=S)[C * q:C * q + C, b, h0:h0 + 16]
                                 ).then_inc(stored, 16)
            sp.wait_ge(stored, 16 * 8 * Q)

        @block.gpsimd
        def _(pool):
            chain = [0]

            def step(ins):
                chain[0] += 1
                ins.then_inc(pool_chain, 1)
                pool.wait_ge(pool_chain, chain[0])

            nc.gpsimd.memset(y8[:, :, :, :, :], 0.0).then_inc(y8_zero, 1)
            nc.gpsimd.memset(gc, 0.0)
            nc.gpsimd.memset(hst, 0.0).then_inc(zeroed, 1)
            nc.gpsimd.nop().then_inc(h_stored, 2)

            def stage_x(rows, rows_b, par):
                nc.gpsimd.tensor_copy(xst[:, par, 0].rearrange("p f (b t) -> p f b t", b=2),
                                      xg[:, :, rows, :].rearrange("p b f t -> p f b t"))
                nc.gpsimd.tensor_copy(xst[:, par, 1, ::-1].rearrange("p f (b t) -> p f b t", b=2),
                                      xg[:, :, rows_b, :].rearrange("p b f t -> p f b t")).then_inc(xst_ready, 1)

            def store_h(rows, rows_b, par, count, stores, staged):
                for b in range(2):
                    pool.wait_ge(h_ready[b], count)
                pool.wait_ge(xst_ready, staged)
                pool.sem_inc(pool_turn, 1)
                tile = hst[:, par * GROUP:(par + 1) * GROUP]
                nc.gpsimd.tensor_copy(hall[0:DQ, rows].rearrange("p f b t -> p f (b t)"), tile[0:DQ]).then_inc(hf_stored, 1)
                pool.wait_ge(hf_stored, stores)
                pool.sem_inc(pool_turn, 1)
                nc.gpsimd.tensor_copy(hall[DQ:P, rows_b].rearrange("p f b t -> p f (b t)"), tile[DQ:P, ::-1]
                                      ).then_inc(h_stored, 1)

            pool.wait_ge(xg_ready, 2)
            for n in range(2):
                stage_x(ds(n * GROUP, GROUP), ds(S - (n + 1) * GROUP, GROUP), n)
            with pool.Fori(0, NG // 2 - 1) as it:
                for par in range(2):
                    pool.wait_ge(x_used, it * 2 + (par + 1))
                    pool.wait_ge(h_stored, it * 2 + (par + 2))
                    pool.sem_inc(pool_turn, 1)
                    stage_x(ds(it * (2 * GROUP) + (par + 2) * GROUP, GROUP),
                            ds(it * (-2 * GROUP) + (S - (par + 3) * GROUP), GROUP), par)
                    store_h(ds(it * (2 * GROUP) + par * GROUP, GROUP),
                            ds(it * (-2 * GROUP) + (S - (par + 1) * GROUP), GROUP), par,
                            it * (2 * GROUP) + ((par + 1) * GROUP + 1), it * 2 + (par + 1), it * 2 + (par + 3))
            for n in range(NG - 2, NG):
                store_h(ds(n * GROUP, GROUP), ds(S - (n + 1) * GROUP, GROUP), n % 2, (n + 1) * GROUP + 1, n + 1, NG)
                pool.wait_ge(h_stored, 2 + n + 1)
            pool.wait_ge(x_used, NG)
            nc.gpsimd.memset(pad[:, :, 0:PAD:PAD - 1, :], 0.0).then_inc(pad_zero, 1)
            nc.gpsimd.memset(pad[:, :, 1:1 + S, 0:PAD:PAD - 1], 0.0).then_inc(pad_zero, 1)
            pool.wait_ge(part3, 2 + NCH)
            step(nc.gpsimd.memset(wm, 0.0))
            for a in range(2):
                for q in range(Q):
                    s_ = slice(C * q, C * q + C)
                    w3 = wc[s_, a, :].rearrange("p (k o) -> p k o", k=K)
                    nc.gpsimd.tensor_copy(wm[s_, a, q, 0:P].rearrange("p (k o) -> p k o", k=4), w3[:, 0:8:2, :])
                    nc.gpsimd.tensor_copy(wm[s_, a, q, P:2 * P].rearrange("p (k o) -> p k o", k=4), w3[:, 1:8:2, :])
                    last = nc.gpsimd.tensor_copy(wm[s_, a, q, 2 * P:2 * P + C], w3[:, 8, :])
            last.then_inc(wm_ready, 1)
            pool.wait_ge(wm_ready, 1)
            def chunk(a, b, r, g, fresh):
                for par in range(2):
                    if not fresh:
                        pool.wait_ge(y8_ready, r * 2 + (2 * g + par - 1))
                    r4 = ds(r * ROWS + (1 + HROWS * par), HROWS)
                    src = pad[:, b, r4, 1:1 + S] if a == 0 else pad[:, b, 1:1 + S, r4].rearrange("p h w -> p w h")
                    nc.gpsimd.tensor_copy(xc[:, par, :].rearrange("p (r n) -> p r n", r=HROWS), src).then_inc(xc_ready, 1)
            for a in range(2):
                for b in range(2):
                    g0 = a * NCH + b * 8
                    if g0 == 0:
                        chunk(a, b, 0, 0, True)
                    with pool.Fori(1 if g0 == 0 else 0, 8) as r:
                        chunk(a, b, r, g0, False)

        @block.scalar
        def _(act):
            act.dma_start(vecs[:, :], vec).then_inc(misc_in, 16)
            act.dma_start(avgs[:, :, :], avg).then_inc(misc_in, 16)
            act.dma_start(gb_f, gate_bias).then_inc(lstm_in, 16)
            act.dma_start(gi_b, gate_ind.bitcast(BF16)).then_inc(lstm_in, 16)
            act.dma_start(dsc_s, dsc).then_inc(conv_in, 16)
            act.dma_start(f23_s[:, 0:3, :], fus[1]).then_inc(conv_in, 16)
            act.dma_start(cw_s, cw).then_inc(conv_in, 16)
            act.dma_start(fus_s, fus[0]).then_inc(conv_in, 16)
            act.dma_start(pws[:, :, :], pw).then_inc(conv_in, 16)
            act.dma_start(sels[:, :, :], sel.bitcast(BF16)).then_inc(conv_in, 16)
            for a in range(2):
                act.wait_ge(fuse_mm, a + 1)
                nc.scalar.activation(wc[:, a, :], ps[a][:, 0:K * C], ACT.Copy, scale=-1.0).then_inc(fuse_ev, 1)
            act.wait_ge(fuse_mm, 3)
            for n in range(3):
                m = min(4, K - 4 * n) * P
                last = nc.scalar.activation(of[:, K * P + 4 * P * n:K * P + 4 * P * n + m], ps[2 + n][:, 0:m], ACT.Copy)
            nc.scalar.activation(cbias, ps[5][:, 0:1], ACT.Copy).then_inc(fuse_ev, 1)

            def norm_sqrt(i, n):
                act.wait_ge(sqrt_in, i + 1)
                nc.scalar.activation(nt[:, 3, 0:n], nt[:, 2, 0:n], ACT.Sqrt).then_inc(sqrt_out, 1)

            norm_sqrt(GN1, 2)
            def gate_functions(b, j, count):
                act.wait_ge(gates_ready[b], count)
                gates = stream_gates(b, j)
                nc.scalar.activation(sifo[:, b].rearrange("p (g n) -> p g n", g=3), gates[:, 1:4], ACT.Sigmoid)
                nc.scalar.activation(gc[:, b, 0:S], gates[:, 0], ACT.Tanh).then_inc(sig_ready[b], 1)

            def cell_tanh(b, count):
                act.wait_ge(c_ready[b], count)
                nc.scalar.activation(tc_[:, b], gc[:, b, S:2 * S], ACT.Tanh).then_inc(tc_ready[b], 1)

            def act_step(j, count):
                for b in range(2):
                    gate_functions(b, j, count)
                    cell_tanh(b, count)

            with act.Fori(0, S // ACT_UNROLL) as it:
                for st in range(ACT_UNROLL):
                    act_step(st % UNROLL, it * ACT_UNROLL + (st + 1))
            norm_sqrt(GN2, 2)
            nc.scalar.nop().then_inc(conv_ev, 2)
            with act.Fori(0, NCH // 2) as it:
                for par in range(2):
                    act.wait_ge(conv_mm, it * 2 + (par + 1))
                    nc.scalar.activation(acc[:, ds(it * (2 * CH) + par * CH, CH)], ps[par][:, :], ACT.Identity,
                                         bias=cbias[:, 0:1]).then_inc(conv_ev, 1)
            nc.scalar.nop().then_inc(part3, 2)
            for a in range(2):
                norm_sqrt(BNX + a, 1)
                act.wait_ge(norm_done, BNX + a + 1)
                for n in range(4):
                    v = wide[:, a * L + n * (L // 4):a * L + (n + 1) * (L // 4)]
                    nc.scalar.activation(v, v, ACT.Relu, bias=coef[:, BNX + a, 1, 0:1],
                                         scale=coef[:, BNX + a, 0, 0:1]).then_inc(relu_done, 1)
                with act.Fori(0, NCH // 4) as it:
                    for ready, done in ((off_mm, part1), (rest1, part2), (rest2, part3)):
                        for par in range(2):
                            act.wait_ge(ready, it * 2 + (a * NCH // 2 + par + 1))
                            act.sem_inc(act_turn, 1)
                            nc.scalar.activation(ob[a][0:ONE_ROW + 1, ds(it * (4 * CH) + par * 2 * CH, 2 * CH)],
                                                 psum[0:ONE_ROW + 1, par * 2 * CH:(par + 1) * 2 * CH], ACT.Identity,
                                                 bias=vecs[0:ONE_ROW + 1, V_PWB + a:V_PWB + a + 1]).then_inc(done, 1)
            with act.Fori(0, 2 * NCH) as g:
                for par in range(2):
                    for i in range(HATS):
                        act.wait_ge(d_ready, g * (2 * HATS) + (par * HATS + i + 1))
                        nc.scalar.activation(hat_tile(par, i), ps[D_BANK[i % ND]].rearrange("p (q n) -> p q n", q=2),
                                             ACT.Abs).then_inc(d_read, 1)
            norm_sqrt(BNF, 1)
            act.wait_ge(norm_done, BNF + 1)
            for c in range(8):
                v = ds(c * (L // 8), L // 8)
                nc.scalar.activation(fin[:, v], acc[:, v], ACT.Relu, bias=coef[:, BNF, 1, 0:1],
                                     scale=coef[:, BNF, 0, 0:1]).then_inc(fin_relu, 1)

        @block.vector
        def _(dve):
            chain = [0]

            def step(ins):
                chain[0] += 1
                ins.then_inc(link, 1)
                dve.wait_ge(link, chain[0])

            def norm(i, n, eps, gamma, beta):
                v = nc.vector
                m, var = mv[:, 0:n, 0], mv[:, 0:n, 1]
                t = [nt[:, j, 0:n] for j in range(8)]
                sc, sh = coef[:, i, 0, 0:n], coef[:, i, 1, 0:n]
                gm, gv = ps[NORM_BANK][:, 0:n], ps[NORM_BANK][:, 8:8 + n]
                v.tensor_copy(t[0], m).then_inc(mean_in, 1)
                dve.wait_ge(mean_out, i + 1)
                step(v.tensor_copy(t[6], gm))
                step(v.tensor_tensor(t[1], m, t[6], ALU.subtract))
                step(v.tensor_tensor(t[1], t[1], t[1], ALU.mult))
                v.tensor_tensor(t[1], t[1], var, ALU.add).then_inc(dev_in, 1)
                dve.wait_ge(var_out, i + 1)
                v.tensor_scalar(t[2], gv, float(eps), None, ALU.add).then_inc(sqrt_in, 1)
                dve.wait_ge(sqrt_out, i + 1)
                step(v.reciprocal(t[4], t[3]))
                step(v.tensor_tensor(t[5], t[4], t[4], ALU.mult))
                step(v.tensor_tensor(t[5], t[5], t[2], ALU.mult))
                step(v.tensor_scalar(t[5], t[5], -0.5, 1.5, ALU.mult, ALU.add))
                step(v.tensor_tensor(sc, t[4], t[5], ALU.mult))
                if gamma is not None:
                    step(v.tensor_tensor(sc, sc, gamma, ALU.mult))
                step(v.tensor_tensor(t[7], t[6], sc, ALU.mult))
                if beta is None:
                    ins = v.tensor_scalar(sh, t[7], -1.0, None, ALU.mult)
                else:
                    ins = v.tensor_tensor(sh, beta, t[7], ALU.subtract)
                ins.then_inc(norm_done, 1)
                dve.wait_ge(norm_done, i + 1)

            def stats_of(src, b):
                for r in range(NCH // 2):
                    n = b * (NCH // 2) + r
                    last = nc.vector.bn_stats(stats[:, n, :], src(b, r))
                return last

            def aggregate(n):
                for j in range(n):
                    k = NCH // n
                    last = nc.vector.bn_aggr(mv[:, j, :], stats[:, j * k:(j + 1) * k, :])
                step(last)

            flat = lambda t: (lambda b, r: t[:, b * PIX + r * CH:b * PIX + (r + 1) * CH])

            dve.wait_ge(x_in, 16 * 2 * Q)
            stats_of(flat(xs), 0)
            step(stats_of(flat(xs), 1))
            aggregate(2)
            dve.wait_ge(misc_in, 32)
            norm(GN1, 2, GN_EPS, None, None)
            for b in range(2):
                nc.vector.tensor_scalar(xg[:, b], xv[:, b], coef[:, GN1, 0, b:b + 1], coef[:, GN1, 1, b:b + 1],
                                        ALU.mult, ALU.add).then_inc(xg_ready, 1)
            dve.wait_ge(lstm_in, 16 * 5)
            step(nc.vector.tensor_tensor(gb_r, gb_f[:, 0, :], gb_f[:, 1, :], ALU.add))
            step(nc.vector.tensor_copy(gb_1, gb_r))
            step(nc.vector.scalar_tensor_tensor(gb_r, gb_1, vecs[0:12, V_G1:V_G1 + 1], gb_r, ALU.mult, ALU.add))
            step(nc.vector.tensor_copy(gb_2, gb_r))
            nc.vector.scalar_tensor_tensor(gb_b, gb_2, vecs[0:12, V_G2:V_G2 + 1], gb_r,
                                           ALU.mult, ALU.add).then_inc(gb_ready, 1)
            dve.wait_ge(zeroed, 1)
            for b in range(2):
                nc.vector.nop().then_inc(h_ready[b], 1)

            def cell(b, count):
                dve.wait_ge(sig_ready[b], count)
                nc.vector.tensor_tensor(prod[:, b], sifo[:, b, 0:2 * S], gc[:, b], ALU.mult).then_inc(prod_ready[b], 1)
                dve.wait_ge(prod_ready[b], count)
                nc.vector.tensor_tensor(gc[:, b, S:2 * S], prod[:, b, 0:S], prod[:, b, S:2 * S], ALU.add
                                        ).then_inc(c_ready[b], 1)

            def hidden(b, j, count, group=None):
                if group is not None:
                    dve.wait_ge(h_stored, group)
                dve.wait_ge(tc_ready[b], count)
                nc.vector.tensor_tensor(hst[:, j, b * S:(b + 1) * S], sifo[:, b, 2 * S:3 * S], tc_[:, b], ALU.mult
                                        ).then_inc(h_ready[b], 1)

            def dve_step(j, count, group):
                for b in range(2):
                    cell(b, count)
                    hidden(b, j, count, group if b == 0 and j % GROUP == 0 else None)

            with dve.Fori(0, S // UNROLL) as it:
                for st in range(UNROLL):
                    dve_step(st, it * UNROLL + (st + 1), it * 2 + (st // GROUP + 1))
            nc.vector.nop().then_inc(x1_ready, 4)
            with dve.Fori(0, NCH // 2) as it:
                for par in range(2):
                    dve.wait_ge(lin_ready, it * 2 + (par + 1))
                    for b in range(2):
                        xr = xv[:, b, ds(it * 8 + 4 * par, 4), :]
                        nc.vector.scalar_tensor_tensor(
                            xr, ps[4 + par][:, :].rearrange("p (f b t) -> p b f t", f=4, b=2)[:, b],
                            vecs[:, V_BLIN:V_BLIN + 1], xr, ALU.add, ALU.add).then_inc(x1_ready, 1)
            dve.wait_ge(x1_ready, 4 + 2 * NCH)
            stats_of(flat(xs), 0)
            step(stats_of(flat(xs), 1))
            aggregate(2)
            norm(GN2, 2, GN_EPS, None, None)
            dve.wait_ge(pad_zero, 2)
            for b in range(2):
                nc.vector.tensor_scalar(pad[:, b, 1:1 + S, 1:1 + S], xv[:, b], coef[:, GN2, 0, b:b + 1],
                                        coef[:, GN2, 1, b:b + 1], ALU.mult, ALU.add).then_inc(pad_ready, 1)
            dve.wait_ge(pad_ready, 2)
            for a in range(2):
                for t in range(9):
                    for b in range(2):
                        src = pad_rows(b, 0, t // 3, t % 3, S)
                        w = vecs[:, V_DW + 9 * a + t:V_DW + 9 * a + t + 1]
                        if t == 0:
                            ins = nc.vector.tensor_scalar(hv[a][:, b], src, w, vecs[:, V_DWB + a:V_DWB + a + 1],
                                                          ALU.mult, ALU.add)
                        else:
                            dve.wait_ge(dw_done, 18 * a + 2 * t + b - 1)
                            ins = nc.vector.scalar_tensor_tensor(hv[a][:, b], src, w, hv[a][:, b], ALU.mult, ALU.add)
                        ins.then_inc(dw_done, 1)
                dve.wait_ge(dw_done, 18 * (a + 1))
                h = (h_x, h_y)[a]
                stats_of(flat(h), 0)
                step(stats_of(flat(h), 1))
                aggregate(1)
                norm(BNX + a, 1, BN_EPS, vecs[:, V_BNG + a:V_BNG + a + 1], vecs[:, V_BNB + a:V_BNB + a + 1])
            nc.vector.nop().then_inc(out_read, 2)
            dve.wait_ge(y8_zero, 1)

            def hats(r, g, par):
                for i in range(HATS):
                    v = hat_tile(par, i)
                    dve.wait_ge(d_read, r * (2 * HATS) + (g * 2 * HATS + par * HATS + i + 1))
                    nc.vector.tensor_scalar(v, v, 1.0, 1.0, ALU.min, ALU.subtract).then_inc(v_ready, 1)
                    if i % 2 == 1 and i > 1:
                        evac_y(r, g, par, i // 2 - 1)
                evac_y(r, g, par, 3)
                dve.wait_ge(y8_ready, r * 2 + (2 * g + par + 1))
                for e in range(2):
                    last = nc.vector.tensor_copy(
                        y8[S * e:S * e + S, par, e:Q:2, :, :],
                        ps[Y8_BANK][S * e:S * e + S, 0:2 * HROWS * C].rearrange("p (q r m) -> p q r m", q=2, r=HROWS))
                last.then_inc(y8_read, 1)

            def evac_y(r, g, par, q):
                dve.wait_ge(y_ready, r * (2 * Q) + (g * 2 * Q + par * Q + q + 1))
                nc.vector.tensor_copy(yt[:, par, q, :, :], ps[Y_BANK[q % 2]].rearrange("p (r m) -> p r m", r=HROWS)
                                      ).then_inc(y_read, 1)

            def gather(a, b, r, par, count):
                r4 = ds(r * ROWS + HROWS * par, HROWS)
                v = accv[:, b, r4, :] if a == 0 else accv[:, b, :, r4].rearrange("p h w -> p w h")
                dve.wait_ge(out_ready, count)
                nc.vector.tensor_tensor(v, ps[O_BANK[par]][:, 0:SL].rearrange("p (r n) -> p r n", r=HROWS), v,
                                        ALU.add).then_inc(out_read, 1)

            dve.wait_ge(part3, 2 + NCH)
            for a in range(2):
                for b in range(2):
                    g0 = a * NCH + b * 8
                    def chunk(r, rprev, ahead):
                        hats(r, g0, 0)
                        if ahead:
                            gather(a, b, rprev, 1, r * 2 + 2 * g0)
                        elif g0:
                            gather((g0 // 8 - 1) // 2, (g0 // 8 - 1) % 2, 7, 1, 2 * g0)
                        hats(r, g0, 1)
                        gather(a, b, r, 0, r * 2 + (2 * g0 + 1))
                    chunk(0, None, False)
                    with dve.Fori(1, 8) as r:
                        chunk(r, r - 1, True)
            gather(1, 1, 7, 1, 2 * 2 * NCH)
            dve.wait_ge(out_read, 2 + 2 * 2 * NCH)
            stats_of(flat(acc), 0)
            step(stats_of(flat(acc), 1))
            aggregate(1)
            norm(BNF, 1, BN_EPS, vecs[:, V_FG:V_FG + 1], vecs[:, V_FB:V_FB + 1])
            for c in range(8):
                v = ds(c * (L // 8), L // 8)
                dve.wait_ge(fin_relu, c + 1)
                nc.vector.tensor_tensor(fin[:, v], fin[:, v], xs[:, v], ALU.add).then_inc(fin_ready, 1)

        @block.tensor
        def _(pe):
            mm = nc.tensor.matmul

            def norm_mm(i, n):
                m = avgs[:, 0 if i <= GN2 else 1, :]
                pe.wait_ge(mean_in, i + 1)
                mm(ps[NORM_BANK][:, 0:n], m, nt[:, 0, 0:n], start=True, stop=True).then_inc(mean_out, 1)
                pe.wait_ge(dev_in, i + 1)
                mm(ps[NORM_BANK][:, 8:8 + n], m, nt[:, 1, 0:n], start=True, stop=True).then_inc(var_out, 1)

            pe.wait_ge(conv_in, 16 * 6)
            for a in range(2):
                for k in range(K):
                    last = mm(ps[a][:, k * C:(k + 1) * C], dsc_s[:, a, k, :], f23_s[:, a, :], start=(k == 0), stop=(k == K - 1))
                last.then_inc(fuse_mm, 1)
            for t in range(9):
                last = mm(ps[2 + t // 4][:, (t % 4) * P:(t % 4 + 1) * P], cw_s[:, t, :], fus_s, start=(t % 4 == 0), stop=(t % 4 == 3 or t == 8))
            pe.wait_ge(misc_in, 32)
            mm(ps[5][:, 0:1], fus_s, vecs[:, V_CONVB:V_CONVB + 1], start=True, stop=True).then_inc(fuse_mm, 1)
            norm_mm(GN1, 2)

            def gates_x(b, g, par, group):
                bank = ps[4 * par + 2 * b + g // 2]
                if b == 0 and g == 0:
                    pe.wait_ge(xst_ready, group)
                if g % 2 == 0:
                    mm(bank[:, :], gb_b, gi_b[:, g * GROUP * S:(g + 2) * GROUP * S], start=True, stop=False)
                for d in range(2):
                    last = mm(bank[DQ * d:DQ * d + DQ, (g % 2) * GROUP * S:(g % 2 + 1) * GROUP * S], wx_s[:, d, g, :],
                              xst[:, par, d, :, b * S:(b + 1) * S], start=False, stop=(g % 2 == 1))
                if b == 1 and g == 3:
                    last.then_inc(x_used, 1)

            def gates_h(b, j, count):
                pe.wait_ge(h_ready[b], count)
                pe.sem_inc(pe_turn, 1)
                gates = stream_gates(b, j)
                for g in range(4):
                    for d in range(2):
                        half = slice(DQ * d, DQ * d + DQ)
                        last = mm(gates[half, g], whh_s[:, g, half],
                                  hst[:, (j - 1) % UNROLL, b * S:(b + 1) * S], start=False, stop=True,
                                  skip_group_check=True)
                last.then_inc(gates_ready[b], 1)

            pe.wait_ge(lstm_in, 16 * 5)
            pe.wait_ge(gb_ready, 1)
            pe.wait_ge(fuse_ev, 3)
            for b in range(2):
                for g in range(4):
                    gates_x(b, g, 0, 1)

            def pe_step(j, count, group):
                for b in range(2):
                    gates_h(b, j, count)
                    if group is not None:
                        gates_x(b, j % GROUP, 1 - j // GROUP, group)

            for st in range(UNROLL):
                pe_step(st, st + 1, st // GROUP + 2)
            with pe.Fori(1, NG // 2 - 1) as it:
                for st in range(UNROLL):
                    pe_step(st, it * UNROLL + (st + 1), it * 2 + (st // GROUP + 2))
            for st in range(UNROLL):
                pe_step(st, S - UNROLL + st + 1, NG if st < GROUP else None)
            pe.wait_ge(h_stored, 2 + NG)
            with pe.Fori(0, NCH // 2) as it:
                for par in range(2):
                    pe.wait_ge(x1_ready, it * 4 + (2 * par + 2))
                    mm(ps[4 + par], wlin_s, seq[:, ds(it * (8 * SEQ) + 4 * par * SEQ, 4 * SEQ)], start=True, stop=True
                       ).then_inc(lin_ready, 1)
            norm_mm(GN2, 2)
            pe.wait_ge(pad_ready, 2)
            def conv(b, lo, hi):
                with pe.Fori(lo, hi) as it:
                    for par in range(2):
                        pe.wait_ge(conv_ev, it * 2 + (8 * b + par + 1))
                        for t in range(9):
                            last = mm(ps[par], cwf[:, t, :], pad_rows(b, it * (2 * ROWS) + ROWS * par, t // 3, t % 3, ROWS),
                                      start=(t == 0), stop=(t == 8))
                        last.then_inc(conv_mm, 1)
            conv(0, 0, 4)
            conv(1, 0, CONV_SPLIT)
            norm_mm(BNX, 1)
            conv(1, CONV_SPLIT, 4)
            pe.wait_ge(conv_ev, 2 + NCH)
            pe.wait_ge(dmask_in, 16)
            for a in range(2):
                if a == 1:
                    norm_mm(BNY, 1)
                pe.wait_ge(relu_done, 4 * (a + 1))
                for b in range(2):
                    with pe.Fori(0, 2) as it:
                        for n in range(4):
                            if n % 2 == 0:
                                pe.wait_ge(part3, it * 2 + (a * NCH // 2 + 4 * b + n // 2 + 1))
                            r0 = ds(it * (4 * ROWS) + ROWS * n, ROWS)
                            rhs = hv[a][:, b, r0, :] if a == 0 else hv[a][:, b, :, r0].rearrange("p h w -> p w h")
                            last = mm(ps[n][0:NROW, :], pws[:, a, :], rhs, start=True, stop=True)
                            if n % 2 == 1:
                                last.then_inc(off_mm, 1)
                        for m, (ready, done) in enumerate(((part1, rest1), (part2, rest2))):
                            for n in range(4):
                                if n % 2 == 0:
                                    pe.wait_ge(ready, it * 2 + (a * NCH // 2 + 4 * b + n // 2 + 1))
                                last = mm(ps[n][0:NROW, :], dmask[:, m, :],
                                          ob[a][0:ONE_ROW + 1, ds(it * (4 * CH) + (8 * b + n) * CH, CH)],
                                          start=False, stop=True, skip_group_check=True)
                                if n % 2 == 1:
                                    last.then_inc(done, 1)
            def dist(s, slots, par, off, i):
                if not (isinstance(s, int) and (s + slots) * HATS + i < ND):
                    pe.wait_ge(d_read, s * HATS + (slots * HATS + i - ND + 1))
                for e in range(2):
                    k = 4 * Q + e if i == 8 else 4 * (2 * (i % 2) + e) + i // 2
                    last = mm(ps[D_BANK[i % ND]][:, e * SL:(e + 1) * SL], sels[:, k, :], offs[0:NROW, off],
                              start=(e == 0), stop=(e == 1))
                last.then_inc(d_ready, 1)

            def project(a, s, slots, par, q, r):
                x_r = xc[:, par, r * S:(r + 1) * S]
                if r == 0 and not (isinstance(s, int) and (s + slots) * Q + q < 2):
                    pe.wait_ge(y_read, s * Q + (slots * Q + q - 1))
                for e in range(2):
                    last = mm(ps[Y_BANK[q % 2]][S * e:S * e + S, r * P:(r + 1) * P], x_r, wm[:, a, q, e * P:(e + 1) * P],
                              start=(r == 0), stop=(r == HROWS - 1))
                if r == HROWS - 1:
                    last.then_inc(y_ready, 1)
                if q == 0 and r == 0 and not (isinstance(s, int) and s + slots < 1):
                    pe.wait_ge(y8_read, s + slots)
                e, n = q % 2, (q // 2) * HROWS + r
                last = mm(ps[Y8_BANK][S * e:S * e + S, n * C:(n + 1) * C], x_r, wm[:, a, q, 2 * P:2 * P + C],
                          start=(n == 0), stop=(n == 2 * HROWS - 1))
                if q == Q - 1 and r == HROWS - 1:
                    last.then_inc(y8_ready, 1)

            GROUPS = HROWS * 5
            STEPS = Q * HROWS
            LEAD = 4

            def product(par, group):
                r, k = group // 5, group % 5
                cols = slice(r * S, (r + 1) * S)
                for q in range(Q):
                    w, v = ((y8[:, par, q, r, :], v8[:, par, q // 2, cols]) if k == 4 else
                            (yt[:, par, q, r, k * C:(k + 1) * C], vt[:, par, k, q, cols]))
                    last = mm(ps[O_BANK[par]][C * q:C * q + C, cols], w, v, start=(group == 0), stop=(group == GROUPS - 1))
                if group == GROUPS - 1:
                    last.then_inc(out_ready, 1)

            def slot(a, s, slots, par, off):
                for i in range(STEPS):
                    if off is not None:
                        nslots = 0 if slots is None else slots + 1
                        if i == 0:
                            pe.wait_ge(xc_ready, s + (nslots + 1))
                        if i in HAT_STEP:
                            dist(s, nslots, 1 - par, off, HAT_STEP.index(i))
                        project(a, s, nslots, 1 - par, i // HROWS, i % HROWS)
                    if slots is not None and i >= LEAD:
                        if i == LEAD:
                            pe.wait_ge(v_ready, s * HATS + (slots + 1) * HATS)
                            pe.wait_ge(y_read, s * Q + (slots + 1) * Q)
                            pe.wait_ge(y8_read, s + (slots + 1))
                            pe.wait_ge(out_read, s + (slots + 1))
                        j, n = i - LEAD, STEPS - LEAD
                        for group in range(j * GROUPS // n, (j + 1) * GROUPS // n):
                            product(par, group)

            pe.wait_ge(pos_in, 32)
            pe.wait_ge(part3, 2 + NCH)
            pe.wait_ge(wm_ready, 1)
            for a in range(2):
                s0 = 2 * a * NCH
                slot(a, s0, None, 1, ds(a * L, SL))
                with pe.Fori(0, NCH - 1) as g:
                    for par in range(2):
                        slot(a, g * 2, s0 + par, par, ds(g * CH + (a * L + (par + 1) * SL), SL))
                slot(a, 2 * NCH - 2, s0, 0, ds(a * L + L - SL, SL))
                slot(a, 2 * NCH - 2, s0 + 1, 1, None)
            norm_mm(BNF, 1)


def layout(inputs):
    import numpy as np
    f = np.float32
    g = {k: np.asarray(v) for k, v in inputs.items()}
    order = (2, 0, 1, 3)
    wx = np.zeros((P, 2, 4, DQ), f)
    whh = np.zeros((P, 4, P), f)
    wlin = np.zeros((P, P), f)
    gb = np.zeros((12, 2, P), f)
    for q in range(Q):
        for d, n in enumerate("fb"):
            hid = slice(q * HID, (q + 1) * HID)
            col = slice(d * DQ + q * HID, d * DQ + (q + 1) * HID)
            wih, wh = g[f"L0_conv_W_ih_{n}"], g[f"L0_conv_W_hh_{n}"]
            for j, t in enumerate(order):
                wx[q * 32:(q + 1) * 32, d, j, hid] = wih[t * HID:(t + 1) * HID].T
                whh[col, j, col] = wh[t * HID:(t + 1) * HID].T
                for p in range(PARTS):
                    gb[4 * p + j, 0, col] = g[f"L0_conv_b_ih_{n}"][t * HID:(t + 1) * HID]
                    gb[4 * p + j, 1, col] = g[f"L0_conv_b_hh_{n}"][t * HID:(t + 1) * HID]
            wlin[col, q * 32:(q + 1) * 32] = g["L0_conv_W_lin"][:, d * HID:(d + 1) * HID].T
    gi = np.zeros((12, 4 * GROUP * S), f)
    for p in range(PARTS):
        for j in range(4):
            gi[4 * p + j, j * GROUP * S:(j + 1) * GROUP * S] = 1
    cw = np.zeros((P, K, P), f)
    fus = np.zeros((P, P), f)
    fw = g["L1_conv_fus_w"][:, :, 0, 0]
    for q in range(Q):
        s = slice(q * 32, (q + 1) * 32)
        for t in range(9):
            cw[s, t, s] = g["L1_conv_conv_w"][:, :, t // 3, t % 3]
        fus[s, s] = fw[:, 0:32].T
    f23 = np.zeros((C, 3, C), f)
    f23[:, 0] = fw[:, 32:64].T
    f23[:, 1] = fw[:, 64:96].T
    dsc = np.zeros((C, 2, K, P), f)
    pw = np.zeros((P, 2, NROW), f)
    vec = np.zeros((P, NVEC), f)
    for a, n in enumerate("xy"):
        w = g[f"L1_conv_dsc{n}_w"]
        pww, pwb = g[f"L1_conv_off{n}_pw_w"][:, :, 0, 0], g[f"L1_conv_off{n}_pw_b"]
        for q in range(Q):
            s = slice(q * 32, (q + 1) * 32)
            for k in range(K):
                dsc[:, a, k, s] = w[:, :, k]
            for p in range(PARTS):
                r = p * NOFF + q * K
                pw[s, a, r:r + K] = pww.T
                vec[r:r + K, V_PWB + a] = pwb
            vec[s, V_DWB + a] = g[f"L1_conv_off{n}_dw_b"]
            vec[s, V_BNG + a] = g[f"L1_conv_off{n}_bn_g"]
            vec[s, V_BNB + a] = g[f"L1_conv_off{n}_bn_b"]
            vec[s, V_DW + 9 * a:V_DW + 9 * a + 9] = g[f"L1_conv_off{n}_dw_w"].reshape(C, 9)
        vec[ONE_ROW, V_PWB + a] = 1
    for q in range(Q):
        s = slice(q * 32, (q + 1) * 32)
        vec[s, V_BLIN] = g["L0_conv_b_lin"]
        vec[s, V_CONVB] = g["L1_conv_conv_b"]
        vec[s, V_FG] = g["L1_conv_fus_bn_g"]
        vec[s, V_FB] = g["L1_conv_fus_bn_b"]
    vec[4:12, V_G1] = -1
    vec[8:12, V_G2] = -1
    ch = np.arange(P)
    avg = np.zeros((P, 2, P), f)
    avg[:, 0] = 0.5 * (ch[:, None] // 2 == ch[None] // 2)
    avg[:, 1] = 0.25 * (ch[:, None] % C == ch[None] % C)
    sel = np.zeros((NROW, NSEL, P), f)
    for n in range(NSEL):
        for e in range(2):
            q, k = (n // 4, 2 * (n % 4) + e) if n < 4 * Q else (2 * (n - 4 * Q) + e, 8)
            for p in range(PARTS):
                sel[p * NOFF + q * K + k, n, e * S:(e + 1) * S] = 1
            sel[ONE_ROW, n, e * S:(e + 1) * S] = -np.arange(S)
            sel[ONE_ROW + 1, n, e * S:(e + 1) * S] = 1
    dm = np.zeros((ONE_ROW + 1, 2, NROW), f)
    for m in range(2):
        rows = np.arange((m + 1) * NOFF, ONE_ROW)
        dm[rows, m, rows] = -1
    pos = np.tile(np.arange(S), L // S)[None].astype(f)
    bits = lambda a: (a.view(np.uint32) >> 16).astype(np.uint16)
    return dict(x=g["x"], wx=wx, whh=whh, wlin=wlin, gate_bias=gb, gate_ind=bits(gi), cw=cw, fus=fus, f23=f23,
                dsc=dsc, pw=pw, dm=bits(dm), vec=vec, avg=avg, sel=bits(sel), pos=bits(pos))


def kernel(**inputs):
    import numpy as _np
    import concourse.bacc as _bacc
    from concourse import mybir as _mybir
    from concourse.bass_utils import run_bass_kernel_spmd as _run

    nc = _bacc.Bacc("TRN2", target_bir_lowering=False, num_devices=1)
    arrays, args = {}, {}
    for name, a in layout(inputs).items():
        a = _np.ascontiguousarray(a)
        arrays[f"in_{name}_dram"] = a
        args[name] = nc.dram_tensor(f"in_{name}_dram", a.shape, _mybir.dt.from_np(a.dtype), kind="ExternalInput").ap()
    args["fus"] = (args["fus"], args.pop("f23"))
    out = nc.dram_tensor("out_0_dram", (2 * Q, C, S, S), _mybir.dt.float32, kind="ExternalOutput").ap()
    build(nc, out=out, **args)
    r = _run(nc, [arrays], core_ids=[0])
    return r.results[0]["out_0_dram"]
```

```python
import concourse.bass as bass
from concourse import mybir
from contextlib import ExitStack

F32 = mybir.dt.float32
BF16 = mybir.dt.bfloat16
P = 128
Q = 4
C = 32
S = 64
PIX = S * S
L = 2 * PIX
HID = 16
K = 9
SEQ = 2 * S
DQ = Q * HID
GROUP = 4
NG = S // GROUP
ROWS = 8
CH = ROWS * S
NCH = L // CH
PAD = S + 2
PARTS = 3
NOFF = Q * K
ONE_ROW = PARTS * NOFF
NROW = ONE_ROW + 2
HROWS = ROWS // 2
SL = HROWS * S
NSEL = Q * 4 + 2
GN_EPS = 1e-5
BN_EPS = 1e-5
GN1, GN2, BNX, BNY, BNF = range(5)

(V_BLIN, V_CONVB, V_FG, V_FB, V_G1, V_G2) = range(6)
V_DWB, V_BNG, V_BNB, V_PWB = 6, 8, 10, 12
V_DW = 14
NVEC = V_DW + 18


def build(nc, x, wx, whh, wlin, gate_bias, gate_ind, cw, fus, dsc, pw, dm, vec, avg, sel, pos, out):
    ACT = mybir.ActivationFunctionType
    ALU = mybir.AluOpType
    AX = mybir.AxisListType
    ds = bass.ds
    ctx = ExitStack()
    with ctx:
        def sb(name, shape, dt=F32):
            return ctx.enter_context(nc.sbuf_tensor(name, shape, dt))

        def sem(name):
            return ctx.enter_context(nc.semaphore(name))

        xs = sb("xs", [P, L])
        img = sb("img", [P, 2 * PAD * PAD])
        seq = sb("seq", [P, L + P])
        wide = sb("wide", [P, 2 * L])
        offs = sb("offs", [P, 2 * L], BF16)
        wc = sb("wc", [P, 2, K * C])
        vecs = sb("vecs", [P, NVEC])
        avgs = sb("avgs", [P, 2, P])
        sels = sb("sels", [NROW, NSEL, P], BF16)
        pws = sb("pws", [P, 2, NROW])
        y8 = sb("y8", [P, 2, Q, HROWS, C])
        stats = sb("stats", [P, NCH, 6])
        small = sb("small", [P, 41])
        mv = small[:, 0:4].rearrange("p (n a) -> p n a", a=2)
        nt = small[:, 4:20].rearrange("p (a n) -> p a n", n=2)
        coef = small[:, 20:40].rearrange("p (i a n) -> p i a n", a=2, n=2)
        cbias = small[:, 40:41]
        psum = ctx.enter_context(nc.psum_tensor("psum", [P, 8 * CH], F32))
        ps = [psum[:, i * CH:(i + 1) * CH] for i in range(8)]

        xv = xs[:, :].rearrange("p (b f t) -> p b f t", b=2, f=S)
        xg = img[:, 0:L].rearrange("p (b f t) -> p b f t", b=2, f=S)
        pad = img[:, :].rearrange("p (b h w) -> p b h w", b=2, h=PAD)
        acc = seq[:, 0:L]
        hall = seq[:, 0:L].rearrange("p (f b t) -> p f b t", f=S, b=2)
        accv = acc.rearrange("p (b h w) -> p b h w", b=2, h=S)

        o = 0
        def region(n):
            nonlocal o
            o += n
            return wide[:, o - n:o]
        wx_s = region(2 * 4 * DQ).rearrange("p (d g m) -> p d g m", d=2, g=4)
        whh_s = region(4 * P).rearrange("p (g m) -> p g m", g=4)
        wlin_s = region(P)
        gb_f = region(2 * P)[0:12, :].rearrange("p (a m) -> p a m", a=2)
        gb_r = region(P)[0:12, :]
        gb_1 = region(P // 2)[0:12, :].bitcast(BF16)
        gb_2 = region(P // 2)[0:12, :].bitcast(BF16)
        gb_b = region(P // 2)[0:12, :].bitcast(BF16)
        gi_b = region(2 * GROUP * S)[0:12, :].bitcast(BF16)
        gc = region(2 * 2 * S).rearrange("p (b n) -> p b n", b=2)
        sifo = region(2 * 3 * S).rearrange("p (b n) -> p b n", b=2)
        prod = region(2 * 2 * S).rearrange("p (b n) -> p b n", b=2)
        tc_ = region(2 * S).rearrange("p (b n) -> p b n", b=2)
        hst = region(2 * GROUP * SEQ).rearrange("p (s n) -> p s n", s=2 * GROUP)
        xst = region(2 * 2 * GROUP * SEQ).rearrange("p (s d f n) -> p s d f n", s=2, d=2, f=GROUP)
        dsc_s = region(2 * K * P)[0:C, :].rearrange("p (a k m) -> p a k m", a=2, k=K)
        f23_s = region(3 * C)[0:C, :].rearrange("p (a m) -> p a m", a=3)
        assert o <= 2 * L
        h_x = wide[:, 0:L]
        h_y = wide[:, L:2 * L]
        hxv = h_x.rearrange("p (b h w) -> p b h w", b=2, h=S)
        hyv = h_y.rearrange("p (b h w) -> p b h w", b=2, h=S)
        hv = (hxv, hyv)

        o = 0
        wm = region(2 * Q * K * C).rearrange("p (a q n) -> p a q n", a=2, q=Q)
        xc = region(2 * SL).rearrange("p (a n) -> p a n", a=2)
        vt = region(2 * 4 * Q * SL).rearrange("p (a k q n) -> p a k q n", a=2, k=4, q=Q)
        v8 = region(2 * 2 * SL).rearrange("p (a q n) -> p a q n", a=2, q=2)
        yt = region(2 * Q * HROWS * P).rearrange("p (a q r m) -> p a q r m", a=2, q=Q, r=HROWS)
        assert o <= 2 * L
        fin = h_y

        of = offs[:, :].bitcast(F32)
        stats_y = of[:, 0:2 * NCH * 6].rearrange("p (n s) -> p n s", s=6)
        cw_s = of[:, 0:K * P].rearrange("p (k m) -> p k m", k=K)
        cwf = of[:, K * P:2 * K * P].rearrange("p (k m) -> p k m", k=K)
        fus_s = of[:, 2 * K * P:2 * K * P + P]
        dmask = seq[0:ONE_ROW + 1, L:L + NROW].bitcast(BF16).rearrange("p (a n) -> p a n", a=2)
        dwp = of[:, L // 2:L // 2 + (K - 1) * CH].rearrange("p (t n) -> p t n", t=K - 1)
        ob = [offs[:, a * L:(a + 1) * L] for a in range(2)]

        x_in = [sem(f"x_in{b}") for b in range(2)]; lstm_in = sem("lstm_in"); conv_in = sem("conv_in"); misc_in = sem("misc_in")
        pos_in = sem("pos_in"); dmask_in = sem("dmask_in"); act_turn = sem("act_turn"); stored = sem("stored")
        mean_in = sem("mean_in"); mean_out = sem("mean_out"); dev_in = sem("dev_in")
        var_out = sem("var_out"); sqrt_in = sem("sqrt_in"); sqrt_out = sem("sqrt_out")
        norm_done = sem("norm_done"); link = sem("link")
        xg_ready = sem("xg_ready"); gb_ready = sem("gb_ready")
        gates_ready = [sem(f"gates_ready{b}") for b in range(2)]
        sig_ready = [sem(f"sig_ready{b}") for b in range(2)]
        prod_ready = [sem(f"prod_ready{b}") for b in range(2)]
        c_ready = [sem(f"c_ready{b}") for b in range(2)]
        tc_ready = [sem(f"tc_ready{b}") for b in range(2)]
        h_ready = [sem(f"h_ready{b}") for b in range(2)]
        xst_ready = sem("xst_ready"); x_used = sem("x_used")
        hf_stored = sem("hf_stored"); h_stored = sem("h_stored"); h_last = sem("h_last")
        pool_turn = sem("pool_turn"); pe_turn = sem("pe_turn")
        lin_ready = sem("lin_ready"); x1_ready = sem("x1_ready")
        fuse_mm = sem("fuse_mm"); zeroed = sem("zeroed"); fuse_ev = sem("fuse_ev"); pool_chain = sem("pool_chain")
        pad_zero = sem("pad_zero"); pad_ready = [sem(f"pad_ready{b}") for b in range(2)]
        conv_mm = sem("conv_mm"); conv_ev = sem("conv_ev")
        dw_done = sem("dw_done"); dwp_ready = sem("dwp_ready"); dwp_used = sem("dwp_used"); relu_done = sem("relu_done")
        off_mm = sem("off_mm"); part1 = sem("part1"); rest1 = sem("rest1")
        part2 = sem("part2"); rest2 = sem("rest2"); part3 = sem("part3")
        relu_v = sem("relu_v"); part1_v = sem("part1_v"); part2_v = sem("part2_v"); part3_v = sem("part3_v")
        wm_ready = sem("wm_ready"); y8_zero = sem("y8_zero")
        xc_ready = sem("xc_ready"); d_ready = sem("d_ready"); d_read = sem("d_read"); v_ready = sem("v_ready")
        y_ready = sem("y_ready"); y_read = sem("y_read"); y8_ready = sem("y8_ready"); y8_read = sem("y8_read")
        out_ready = sem("out_ready"); out_read = sem("out_read"); fin_relu = sem("fin_relu"); fin_ready = sem("fin_ready")

        def pad_rows(b, row, dy, dx, n):
            return pad[:, b, ds(row + dy, n), dx:dx + S]

        def stream_gates(b, j):
            c0 = (4 * (j // GROUP) + 2 * b) * CH
            return psum[:, c0:c0 + 2 * CH].rearrange("p (g f t) -> p g f t", g=4, f=GROUP)[:, :, j % GROUP]

        UNROLL = 2 * GROUP

        ACT_UNROLL = 2 * UNROLL

        HATS = 9
        def hat_tile(par, i):
            return v8[:, par, :, :] if i == 8 else vt[:, par, i // 2, 2 * (i % 2):2 * (i % 2) + 2, :]
        HAT_STEP = (0, 1, 3, 4, 6, 7, 9, 10, 12)
        D_BANK, Y_BANK, Y8_BANK, O_BANK = (0, 1, 2), (3, 4), 5, (6, 7)
        ND = 3
        NORM_BANK = 7
        DW_AHEAD = 3
        DVE_CH = 6
        CONV_SPLIT = 2

        block = ctx.enter_context(nc.Block())

        @block.sync
        def _(sp):
            for b in range(2):
                for q in range(Q):
                    sp.dma_start(xv[C * q:C * q + C, b], x[2 * q + b]).then_inc(x_in[b], 16)
            sp.dma_start(wx_s, wx).then_inc(lstm_in, 16)
            sp.dma_start(whh_s, whh).then_inc(lstm_in, 16)
            sp.dma_start(wlin_s, wlin).then_inc(lstm_in, 16)
            sp.wait_ge(lin_ready, NCH)
            sp.dma_start(dmask, dm.bitcast(BF16)).then_inc(dmask_in, 16)
            sp.wait_ge(conv_ev, 2 + NCH)
            for a in range(2):
                if a == 1:
                    sp.wait_ge(dwp_used, (K - 1) * (1 + NCH - DVE_CH))
                sp.dma_start(ob[a][ONE_ROW + 1:ONE_ROW + 2, :], pos.bitcast(BF16)).then_inc(pos_in, 16)
            for c in range(8):
                sp.wait_ge(fin_ready, c + 1)
                b, h0 = c // 4, 16 * (c % 4)
                for q in range(Q):
                    sp.dma_start(out[2 * q + b, :, h0:h0 + 16, :],
                                 fin.rearrange("p (b h w) -> p b h w", b=2, h=S)[C * q:C * q + C, b, h0:h0 + 16]
                                 ).then_inc(stored, 16)
            sp.wait_ge(stored, 16 * 8 * Q)

        @block.gpsimd
        def _(pool):
            chain = [0]

            def step(ins):
                chain[0] += 1
                ins.then_inc(pool_chain, 1)
                pool.wait_ge(pool_chain, chain[0])

            nc.gpsimd.memset(y8[:, :, :, :, :], 0.0).then_inc(y8_zero, 1)
            nc.gpsimd.memset(gc, 0.0)
            nc.gpsimd.memset(hst, 0.0).then_inc(zeroed, 1)
            nc.gpsimd.nop().then_inc(h_stored, 2)

            def stage_x(rows, rows_b, par):
                nc.gpsimd.tensor_copy(xst[:, par, 0].rearrange("p f (b t) -> p f b t", b=2),
                                      xg[:, :, rows, :].rearrange("p b f t -> p f b t"))
                nc.gpsimd.tensor_copy(xst[:, par, 1, ::-1].rearrange("p f (b t) -> p f b t", b=2),
                                      xg[:, :, rows_b, :].rearrange("p b f t -> p f b t")).then_inc(xst_ready, 1)

            def store_h(rows, rows_b, par, count, stores, staged):
                for b in range(2):
                    pool.wait_ge(h_ready[b], count)
                pool.wait_ge(xst_ready, staged)
                pool.sem_inc(pool_turn, 1)
                tile = hst[:, par * GROUP:(par + 1) * GROUP]
                nc.gpsimd.tensor_copy(hall[0:DQ, rows].rearrange("p f b t -> p f (b t)"), tile[0:DQ]).then_inc(hf_stored, 1)
                pool.wait_ge(hf_stored, stores)
                pool.sem_inc(pool_turn, 1)
                nc.gpsimd.tensor_copy(hall[DQ:P, rows_b].rearrange("p f b t -> p f (b t)"), tile[DQ:P, ::-1]
                                      ).then_inc(h_stored, 1)

            pool.wait_ge(xst_ready, 1)
            stage_x(ds(GROUP, GROUP), ds(S - 2 * GROUP, GROUP), 1)
            with pool.Fori(0, NG // 2 - 1) as it:
                for par in range(2):
                    pool.wait_ge(x_used, it * 2 + (par + 1))
                    pool.wait_ge(h_stored, it * 2 + (par + 2))
                    pool.sem_inc(pool_turn, 1)
                    stage_x(ds(it * (2 * GROUP) + (par + 2) * GROUP, GROUP),
                            ds(it * (-2 * GROUP) + (S - (par + 3) * GROUP), GROUP), par)
                    store_h(ds(it * (2 * GROUP) + par * GROUP, GROUP),
                            ds(it * (-2 * GROUP) + (S - (par + 1) * GROUP), GROUP), par,
                            it * (2 * GROUP) + ((par + 1) * GROUP + 1), it * 2 + (par + 1), it * 2 + (par + 3))
            store_h(ds(S - 2 * GROUP, GROUP), ds(GROUP, GROUP), 0, S - GROUP + 1, NG - 1, NG)
            pool.wait_ge(h_stored, 2 + NG - 1)
            pool.wait_ge(x_used, NG)
            nc.gpsimd.memset(pad[:, :, 0:PAD:PAD - 1, :], 0.0).then_inc(pad_zero, 1)
            nc.gpsimd.memset(pad[:, :, 1:1 + S, 0:PAD:PAD - 1], 0.0).then_inc(pad_zero, 1)
            nc.gpsimd.nop().then_inc(dwp_used, K - 1)
            for b, lo, before in ((1, 0, 0), (0, DVE_CH, NCH // 2 - DVE_CH)):
                with pool.Fori(lo, NCH // 2) as c:
                    for t in range(1, K):
                        pool.wait_ge(dwp_ready, c * (K - 1) + (before * (K - 1) + t))
                        pool.wait_ge(dwp_used, c * (K - 1) + ((before + 1) * (K - 1) + t - 1))
                        pool.sem_inc(pool_turn, 1)
                        h = h_y[:, ds(c * CH + b * PIX, CH)]
                        nc.gpsimd.tensor_tensor(h, h, dwp[:, t - 1], ALU.add).then_inc(dwp_used, 1)
            pool.wait_ge(dwp_used, (K - 1) * (1 + NCH - DVE_CH))
            pool.wait_ge(part3, NCH // 2)
            step(nc.gpsimd.memset(wm, 0.0))
            for a in range(2):
                for q in range(Q):
                    s_ = slice(C * q, C * q + C)
                    w3 = wc[s_, a, :].rearrange("p (k o) -> p k o", k=K)
                    nc.gpsimd.tensor_copy(wm[s_, a, q, 0:P].rearrange("p (k o) -> p k o", k=4), w3[:, 0:8:2, :])
                    nc.gpsimd.tensor_copy(wm[s_, a, q, P:2 * P].rearrange("p (k o) -> p k o", k=4), w3[:, 1:8:2, :])
                    last = nc.gpsimd.tensor_copy(wm[s_, a, q, 2 * P:2 * P + C], w3[:, 8, :])
            last.then_inc(wm_ready, 1)
            pool.wait_ge(wm_ready, 1)
            def chunk(a, b, r, g, fresh):
                for par in range(2):
                    if not fresh:
                        pool.wait_ge(y8_ready, r * 2 + (2 * g + par - 1))
                    r4 = ds(r * ROWS + (1 + HROWS * par), HROWS)
                    src = pad[:, b, r4, 1:1 + S] if a == 0 else pad[:, b, 1:1 + S, r4].rearrange("p h w -> p w h")
                    nc.gpsimd.tensor_copy(xc[:, par, :].rearrange("p (r n) -> p r n", r=HROWS), src).then_inc(xc_ready, 1)
            for a in range(2):
                for b in range(2):
                    g0 = a * NCH + b * 8
                    if g0 == 0:
                        chunk(a, b, 0, 0, True)
                    with pool.Fori(1 if g0 == 0 else 0, 8) as r:
                        chunk(a, b, r, g0, False)

        @block.scalar
        def _(act):
            act.dma_start(vecs[:, :], vec).then_inc(misc_in, 16)
            act.dma_start(avgs[:, :, :], avg).then_inc(misc_in, 16)
            act.dma_start(gb_f, gate_bias).then_inc(lstm_in, 16)
            act.dma_start(gi_b, gate_ind.bitcast(BF16)).then_inc(lstm_in, 16)
            def norm_sqrt(i, n):
                act.wait_ge(sqrt_in, i + 1)
                nc.scalar.activation(nt[:, 3, 0:n], nt[:, 2, 0:n], ACT.Sqrt).then_inc(sqrt_out, 1)

            norm_sqrt(GN1, 2)
            act.wait_ge(norm_done, GN1 + 1)
            nc.scalar.activation(xg[:, 1], xv[:, 1], ACT.Identity, bias=coef[:, GN1, 1, 1:2],
                                 scale=coef[:, GN1, 0, 1:2]).then_inc(xg_ready, 1)
            act.dma_start(dsc_s, dsc).then_inc(conv_in, 16)
            act.dma_start(f23_s[:, 0:3, :], fus[1]).then_inc(conv_in, 16)
            act.dma_start(cw_s, cw).then_inc(conv_in, 16)
            act.dma_start(fus_s, fus[0]).then_inc(conv_in, 16)
            act.dma_start(pws[:, :, :], pw).then_inc(conv_in, 16)
            act.dma_start(sels[:, :, :], sel.bitcast(BF16)).then_inc(conv_in, 16)
            def gate_functions(b, j, count):
                act.wait_ge(gates_ready[b], count)
                gates = stream_gates(b, j)
                nc.scalar.activation(sifo[:, b].rearrange("p (g n) -> p g n", g=3), gates[:, 1:4], ACT.Sigmoid)
                nc.scalar.activation(gc[:, b, 0:S], gates[:, 0], ACT.Tanh).then_inc(sig_ready[b], 1)

            def cell_tanh(b, count):
                act.wait_ge(c_ready[b], count)
                nc.scalar.activation(tc_[:, b], gc[:, b, S:2 * S], ACT.Tanh).then_inc(tc_ready[b], 1)

            def act_step(j, count):
                for b in range(2):
                    gate_functions(b, j, count)
                    cell_tanh(b, count)

            with act.Fori(0, S // ACT_UNROLL) as it:
                for st in range(ACT_UNROLL):
                    act_step(st % UNROLL, it * ACT_UNROLL + (st + 1))
            for a in range(2):
                act.wait_ge(fuse_mm, a + 1)
                nc.scalar.activation(wc[:, a, :], ps[a][:, 0:K * C], ACT.Copy, scale=-1.0).then_inc(fuse_ev, 1)
            act.wait_ge(fuse_mm, 3)
            for n in range(3):
                m = min(4, K - 4 * n) * P
                last = nc.scalar.activation(of[:, K * P + 4 * P * n:K * P + 4 * P * n + m], ps[(2, 3, 6)[n]][:, 0:m], ACT.Copy)
            nc.scalar.activation(cbias, ps[6][:, P:P + 1], ACT.Copy).then_inc(fuse_ev, 1)

            norm_sqrt(GN2, 2)
            act.wait_ge(norm_done, GN2 + 1)
            act.wait_ge(pad_zero, 2)
            nc.scalar.activation(pad[:, 1, 1:1 + S, 1:1 + S], xv[:, 1], ACT.Identity, bias=coef[:, GN2, 1, 1:2],
                                 scale=coef[:, GN2, 0, 1:2]).then_inc(pad_ready[1], 1)
            act.wait_ge(pad_ready[1], 1)
            def relu_x():
                act.wait_ge(norm_done, BNX + 1)
                for n in range(4):
                    v = h_x[:, n * (L // 4):(n + 1) * (L // 4)]
                    nc.scalar.activation(v, v, ACT.Relu, bias=coef[:, BNX, 1, 0:1], scale=coef[:, BNX, 0, 0:1]
                                         ).then_inc(relu_done, 1)

            nc.scalar.nop().then_inc(conv_ev, 2)
            def dw_product(b, it, mul, add, t, before=0):
                w = vecs[:, V_DW + 9 + t:V_DW + 10 + t]
                src = pad_rows(b, it * (mul * ROWS) + add * ROWS, t // 3, t % 3, ROWS)
                if t == 0:
                    h = h_y[:, ds(it * (mul * CH) + (add * CH + b * PIX), CH)]
                    nc.scalar.activation(h.rearrange("p (h w) -> p h w", h=ROWS), src, ACT.Identity, bias=vecs[:, V_DWB + 1:V_DWB + 2], scale=w)
                else:
                    act.wait_ge(dwp_used, it * (mul * (K - 1)) + ((add + before) * (K - 1) + t))
                    act.sem_inc(act_turn, 1)
                    nc.scalar.activation(dwp[:, t - 1].rearrange("p (h w) -> p h w", h=ROWS), src, ACT.Copy, scale=w
                                         ).then_inc(dwp_ready, 1)

            def conv_chunk(it, mul, add):
                act.wait_ge(conv_mm, it * mul + (add + 1))
                nc.scalar.activation(acc[:, ds(it * (mul * CH) + add * CH, CH)], ps[add % 2][:, :], ACT.Identity,
                                     bias=cbias[:, 0:1]).then_inc(conv_ev, 1)

            with act.Fori(0, 2) as it:
                for n in range(6):
                    conv_chunk(it, 6, n)
                    for k in range(6 * n, 6 * n + 6):
                        dw_product(1, it, 4, k // K, k % K)
            norm_sqrt(BNX, 1)
            relu_x()
            with act.Fori(DVE_CH, NCH // 2) as it:
                for par in range(2):
                    conv_chunk(it, 2, par)
                    for t in ((0, 1, 2, 3, 4), (5, 6, 7, 8))[par]:
                        dw_product(0, it, 1, 0, t, NCH // 2 - DVE_CH)
            for a in range(2):
                for b in range(2):
                    if a == 0 and b == 1:
                        norm_sqrt(BNY, 1)
                    for ready, done in ((off_mm, part1), (rest1, part2), (rest2, part3)):
                        for n in range(4 - 2 * a):
                            act.wait_ge(ready, 4 * (2 * a + b) + n + 1)
                            nc.scalar.activation(ob[a][0:ONE_ROW + 1, b * PIX + n * 2 * CH:b * PIX + (n + 1) * 2 * CH],
                                                 psum[0:ONE_ROW + 1, n * 2 * CH:(n + 1) * 2 * CH], ACT.Identity,
                                                 bias=vecs[0:ONE_ROW + 1, V_PWB + a:V_PWB + a + 1]).then_inc(done, 1)
            with act.Fori(0, 2 * NCH) as g:
                for par in range(2):
                    for i in range(HATS):
                        act.wait_ge(d_ready, g * (2 * HATS) + (par * HATS + i + 1))
                        nc.scalar.activation(hat_tile(par, i), ps[D_BANK[i % ND]].rearrange("p (q n) -> p q n", q=2),
                                             ACT.Abs).then_inc(d_read, 1)
            norm_sqrt(BNF, 1)
            act.wait_ge(norm_done, BNF + 1)
            for c in range(8):
                v = ds(c * (L // 8), L // 8)
                nc.scalar.activation(fin[:, v], acc[:, v], ACT.Relu, bias=coef[:, BNF, 1, 0:1],
                                     scale=coef[:, BNF, 0, 0:1]).then_inc(fin_relu, 1)

        @block.vector
        def _(dve):
            chain = [0]

            def step(ins):
                chain[0] += 1
                ins.then_inc(link, 1)
                dve.wait_ge(link, chain[0])

            def norm(i, n, eps, gamma, beta):
                v = nc.vector
                m, var = mv[:, 0:n, 0], mv[:, 0:n, 1]
                t = [nt[:, j, 0:n] for j in range(8)]
                sc, sh = coef[:, i, 0, 0:n], coef[:, i, 1, 0:n]
                gm, gv = ps[NORM_BANK][:, 0:n], ps[NORM_BANK][:, 8:8 + n]
                v.tensor_copy(t[0], m).then_inc(mean_in, 1)
                dve.wait_ge(mean_out, i + 1)
                step(v.tensor_copy(t[6], gm))
                step(v.tensor_tensor(t[1], m, t[6], ALU.subtract))
                step(v.tensor_tensor(t[1], t[1], t[1], ALU.mult))
                v.tensor_tensor(t[1], t[1], var, ALU.add).then_inc(dev_in, 1)
                dve.wait_ge(var_out, i + 1)
                v.tensor_scalar(t[2], gv, float(eps), None, ALU.add).then_inc(sqrt_in, 1)
                dve.wait_ge(sqrt_out, i + 1)
                step(v.reciprocal(t[4], t[3]))
                step(v.tensor_tensor(t[5], t[4], t[4], ALU.mult))
                step(v.tensor_tensor(t[5], t[5], t[2], ALU.mult))
                step(v.tensor_scalar(t[5], t[5], -0.5, 1.5, ALU.mult, ALU.add))
                step(v.tensor_tensor(sc, t[4], t[5], ALU.mult))
                if gamma is not None:
                    step(v.tensor_tensor(sc, sc, gamma, ALU.mult))
                step(v.tensor_tensor(t[7], t[6], sc, ALU.mult))
                if beta is None:
                    ins = v.tensor_scalar(sh, t[7], -1.0, None, ALU.mult)
                else:
                    ins = v.tensor_tensor(sh, beta, t[7], ALU.subtract)
                ins.then_inc(norm_done, 1)
                dve.wait_ge(norm_done, i + 1)

            def stats_of(src, b, lo=0, hi=NCH // 2):
                for r in range(lo, hi):
                    n = b * (NCH // 2) + r
                    last = nc.vector.bn_stats(stats[:, n, :], src(b, r))
                return last

            def aggregate(n):
                for j in range(n):
                    k = NCH // n
                    last = nc.vector.bn_aggr(mv[:, j, :], stats[:, j * k:(j + 1) * k, :])
                step(last)

            flat = lambda t: (lambda b, r: t[:, b * PIX + r * CH:b * PIX + (r + 1) * CH])

            dve.wait_ge(x_in[0], 16 * Q)
            stats_of(flat(xs), 0)
            dve.wait_ge(x_in[1], 16 * Q)
            step(stats_of(flat(xs), 1))
            aggregate(2)
            dve.wait_ge(misc_in, 32)
            norm(GN1, 2, GN_EPS, None, None)
            nc.vector.tensor_scalar(xg[:, 0], xv[:, 0], coef[:, GN1, 0, 0:1], coef[:, GN1, 1, 0:1],
                                    ALU.mult, ALU.add).then_inc(xg_ready, 1)
            dve.wait_ge(lstm_in, 16 * 5)
            step(nc.vector.tensor_tensor(gb_r, gb_f[:, 0, :], gb_f[:, 1, :], ALU.add))
            step(nc.vector.tensor_copy(gb_1, gb_r))
            step(nc.vector.scalar_tensor_tensor(gb_r, gb_1, vecs[0:12, V_G1:V_G1 + 1], gb_r, ALU.mult, ALU.add))
            step(nc.vector.tensor_copy(gb_2, gb_r))
            nc.vector.scalar_tensor_tensor(gb_b, gb_2, vecs[0:12, V_G2:V_G2 + 1], gb_r,
                                           ALU.mult, ALU.add).then_inc(gb_ready, 1)
            dve.wait_ge(xg_ready, 2)
            nc.vector.tensor_copy(xst[:, 0, 0].rearrange("p f (b t) -> p f b t", b=2),
                                  xg[:, :, 0:GROUP, :].rearrange("p b f t -> p f b t"))
            nc.vector.tensor_copy(xst[:, 0, 1, ::-1].rearrange("p f (b t) -> p f b t", b=2),
                                  xg[:, :, S - GROUP:S, :].rearrange("p b f t -> p f b t")).then_inc(xst_ready, 1)
            dve.wait_ge(zeroed, 1)
            for b in range(2):
                nc.vector.nop().then_inc(h_ready[b], 1)

            def cell(b, count):
                dve.wait_ge(sig_ready[b], count)
                nc.vector.tensor_tensor(prod[:, b], sifo[:, b, 0:2 * S], gc[:, b], ALU.mult).then_inc(prod_ready[b], 1)
                dve.wait_ge(prod_ready[b], count)
                nc.vector.tensor_tensor(gc[:, b, S:2 * S], prod[:, b, 0:S], prod[:, b, S:2 * S], ALU.add
                                        ).then_inc(c_ready[b], 1)

            def hidden(b, j, count, group=None):
                if group is not None:
                    dve.wait_ge(h_stored, group)
                dve.wait_ge(tc_ready[b], count)
                nc.vector.tensor_tensor(hst[:, j, b * S:(b + 1) * S], sifo[:, b, 2 * S:3 * S], tc_[:, b], ALU.mult
                                        ).then_inc(h_ready[b], 1)

            def dve_step(j, count, group):
                for b in range(2):
                    cell(b, count)
                    hidden(b, j, count, group if b == 0 and j % GROUP == 0 else None)

            with dve.Fori(0, S // UNROLL) as it:
                for st in range(UNROLL):
                    dve_step(st, it * UNROLL + (st + 1), it * 2 + (st // GROUP + 1))
            for b in range(2):
                dve.wait_ge(h_ready[b], S + 1)
            tile = hst[:, GROUP:2 * GROUP]
            nc.vector.tensor_copy(hall[0:DQ, S - GROUP:S].rearrange("p f b t -> p f (b t)"), tile[0:DQ])
            nc.vector.tensor_copy(hall[DQ:P, 0:GROUP].rearrange("p f b t -> p f (b t)"), tile[DQ:P, ::-1]
                                  ).then_inc(h_last, 1)

            def stats_x1(c):
                dve.wait_ge(x1_ready, 4 + 4 * (c + 1))
                for b in range(2):
                    last = nc.vector.bn_stats(stats[:, b * (NCH // 2) + c, :], flat(xs)(b, c))
                return last

            nc.vector.nop().then_inc(x1_ready, 4)
            for n in range(NCH):
                dve.wait_ge(lin_ready, n + 1)
                for b in range(2):
                    xr = xv[:, b, 4 * n:4 * n + 4, :]
                    nc.vector.scalar_tensor_tensor(
                        xr, ps[4 + n % 2][:, :].rearrange("p (f b t) -> p b f t", f=4, b=2)[:, b],
                        vecs[:, V_BLIN:V_BLIN + 1], xr, ALU.add, ALU.add).then_inc(x1_ready, 1)
                if n % 2 == 0 and n > 0:
                    stats_x1(n // 2 - 1)
            dve.wait_ge(x1_ready, 4 + 2 * NCH)
            step(stats_x1(NCH // 2 - 1))
            aggregate(2)
            norm(GN2, 2, GN_EPS, None, None)
            dve.wait_ge(pad_zero, 2)
            nc.vector.tensor_scalar(pad[:, 0, 1:1 + S, 1:1 + S], xv[:, 0], coef[:, GN2, 0, 0:1],
                                    coef[:, GN2, 1, 0:1], ALU.mult, ALU.add).then_inc(pad_ready[0], 1)
            def depthwise(a, lo, hi):
                rows = (S, DVE_CH * ROWS)[a]
                for t in range(lo, hi):
                    for b in range(2 - a):
                        src = pad_rows(b, 0, t // 3, t % 3, rows)
                        dst = hv[a][:, b, 0:rows]
                        w = vecs[:, V_DW + 9 * a + t:V_DW + 9 * a + t + 1]
                        if t == 0:
                            if a == 0:
                                dve.wait_ge(pad_ready[b], 1)
                            ins = nc.vector.tensor_scalar(dst, src, w, vecs[:, V_DWB + a:V_DWB + a + 1],
                                                          ALU.mult, ALU.add)
                        else:
                            dve.wait_ge(dw_done, 18 * a + (2 - a) * (t - 1) + b + 1)
                            ins = nc.vector.scalar_tensor_tensor(dst, src, w, dst, ALU.mult, ALU.add)
                        ins.then_inc(dw_done, 1)

            def norm_offsets(a):
                norm(BNX + a, 1, BN_EPS, vecs[:, V_BNG + a:V_BNG + a + 1], vecs[:, V_BNB + a:V_BNB + a + 1])

            depthwise(0, 0, K)
            dve.wait_ge(dw_done, 18)
            stats_of(flat(h_x), 0)
            step(stats_of(flat(h_x), 1))
            aggregate(1)
            depthwise(1, 0, DW_AHEAD)
            norm_offsets(0)
            depthwise(1, DW_AHEAD, K)
            dve.wait_ge(dw_done, 18 + K)
            stats_of(flat(h_y), 0, 0, DVE_CH)
            dve.wait_ge(dwp_used, (K - 1) * (1 + NCH - DVE_CH))
            stats_of(flat(h_y), 0, DVE_CH)
            step(stats_of(flat(h_y), 1))
            aggregate(1)
            norm_offsets(1)
            for b in range(2):
                step(nc.vector.tensor_scalar(hv[1][:, b], hv[1][:, b], coef[:, BNY, 0, 0:1], coef[:, BNY, 1, 0:1],
                                             ALU.mult, ALU.add))
                nc.vector.tensor_scalar(hv[1][:, b], hv[1][:, b], 0.0, None, ALU.max).then_inc(relu_v, 1)
            for b in range(2):
                for ready, done in ((off_mm, part1_v), (rest1, part2_v), (rest2, part3_v)):
                    for n in range(2, 4):
                        dve.wait_ge(ready, 4 * (2 + b) + n + 1)
                        nc.vector.tensor_scalar(ob[1][0:ONE_ROW + 1, b * PIX + n * 2 * CH:b * PIX + (n + 1) * 2 * CH],
                                                psum[0:ONE_ROW + 1, n * 2 * CH:(n + 1) * 2 * CH],
                                                vecs[0:ONE_ROW + 1, V_PWB + 1:V_PWB + 2], None, ALU.add).then_inc(done, 1)
            nc.vector.nop().then_inc(out_read, 2)
            dve.wait_ge(y8_zero, 1)

            def hats(r, g, par):
                for i in range(HATS):
                    v = hat_tile(par, i)
                    dve.wait_ge(d_read, r * (2 * HATS) + (g * 2 * HATS + par * HATS + i + 1))
                    nc.vector.tensor_scalar(v, v, 1.0, 1.0, ALU.min, ALU.subtract).then_inc(v_ready, 1)
                    if i % 2 == 1 and i > 1:
                        evac_y(r, g, par, i // 2 - 1)
                evac_y(r, g, par, 3)
                dve.wait_ge(y8_ready, r * 2 + (2 * g + par + 1))
                for e in range(2):
                    last = nc.vector.tensor_copy(
                        y8[S * e:S * e + S, par, e:Q:2, :, :],
                        ps[Y8_BANK][S * e:S * e + S, 0:2 * HROWS * C].rearrange("p (r q m) -> p q r m", q=2, r=HROWS))
                last.then_inc(y8_read, 1)

            def evac_y(r, g, par, q):
                dve.wait_ge(y_ready, r * (2 * Q) + (g * 2 * Q + par * Q + q + 1))
                nc.vector.tensor_copy(yt[:, par, q, :, :], ps[Y_BANK[q % 2]].rearrange("p (r m) -> p r m", r=HROWS)
                                      ).then_inc(y_read, 1)

            def sums_of(a, b, r, par):
                r4 = ds(r * ROWS + HROWS * par, HROWS)
                return accv[:, b, r4, :] if a == 0 else accv[:, b, :, r4].rearrange("p h w -> p w h")

            def gather(a, b, r, par, count, before=None):
                dve.wait_ge(out_ready, count)
                if before is not None:
                    dve.wait_ge(out_read, count + 1)
                v = sums_of(a, b, r, par)
                nc.vector.tensor_tensor(v, ps[O_BANK[par]][:, 0:SL].rearrange("p (r n) -> p r n", r=HROWS), v,
                                        ALU.add).then_inc(out_read, 1)
                if before is not None:
                    slot_stats(*before)

            def slot_stats(b, r, par):
                return nc.vector.bn_stats(stats_y[:, ds(r * 2 + (b * NCH + par), 1), :].rearrange("p o s -> p (o s)"),
                                          sums_of(1, b, r, par))

            dve.wait_ge(part3, NCH // 2 + 4)
            for a in range(2):
                for b in range(2):
                    g0 = a * NCH + b * 8
                    def chunk(r, rprev, ahead):
                        hats(r, g0, 0)
                        if ahead:
                            gather(a, b, rprev, 1, r * 2 + 2 * g0, (b, rprev, 0) if a == 1 else None)
                        elif g0:
                            last = (g0 // 8 - 1) % 2
                            gather((g0 // 8 - 1) // 2, last, 7, 1, 2 * g0, (last, 7, 0) if g0 > NCH else None)
                        hats(r, g0, 1)
                        gather(a, b, r, 0, r * 2 + (2 * g0 + 1),
                               None if a == 0 else (b, rprev, 1) if ahead else (0, 7, 1) if b == 1 else None)
                    chunk(0, None, False)
                    with dve.Fori(1, 8) as r:
                        chunk(r, r - 1, True)
            gather(1, 1, 7, 1, 2 * 2 * NCH, (1, 7, 0))
            dve.wait_ge(out_read, 2 + 2 * 2 * NCH)
            step(slot_stats(1, 7, 1))
            step(nc.vector.bn_aggr(mv[:, 0, :], stats_y))
            norm(BNF, 1, BN_EPS, vecs[:, V_FG:V_FG + 1], vecs[:, V_FB:V_FB + 1])
            for c in range(8):
                v = ds(c * (L // 8), L // 8)
                dve.wait_ge(fin_relu, c + 1)
                nc.vector.tensor_tensor(fin[:, v], fin[:, v], xs[:, v], ALU.add).then_inc(fin_ready, 1)

        @block.tensor
        def _(pe):
            mm = nc.tensor.matmul

            def norm_mm(i, n):
                m = avgs[:, 0 if i <= GN2 else 1, :]
                pe.wait_ge(mean_in, i + 1)
                mm(ps[NORM_BANK][:, 0:n], m, nt[:, 0, 0:n], start=True, stop=True).then_inc(mean_out, 1)
                pe.wait_ge(dev_in, i + 1)
                mm(ps[NORM_BANK][:, 8:8 + n], m, nt[:, 1, 0:n], start=True, stop=True).then_inc(var_out, 1)

            pe.wait_ge(misc_in, 32)
            norm_mm(GN1, 2)

            def gates_x(b, g, par, group):
                bank = ps[4 * par + 2 * b + g // 2]
                if b == 0 and g == 0:
                    pe.wait_ge(xst_ready, group)
                if g % 2 == 0:
                    mm(bank[:, :], gb_b, gi_b[:, g * GROUP * S:(g + 2) * GROUP * S], start=True, stop=False)
                for d in range(2):
                    last = mm(bank[DQ * d:DQ * d + DQ, (g % 2) * GROUP * S:(g % 2 + 1) * GROUP * S], wx_s[:, d, g, :],
                              xst[:, par, d, :, b * S:(b + 1) * S], start=False, stop=(g % 2 == 1))
                if b == 1 and g == 3:
                    last.then_inc(x_used, 1)

            def gates_h(b, j, count):
                pe.wait_ge(h_ready[b], count)
                pe.sem_inc(pe_turn, 1)
                gates = stream_gates(b, j)
                for g in range(4):
                    for d in range(2):
                        half = slice(DQ * d, DQ * d + DQ)
                        last = mm(gates[half, g], whh_s[:, g, half],
                                  hst[:, (j - 1) % UNROLL, b * S:(b + 1) * S], start=False, stop=True,
                                  skip_group_check=True)
                last.then_inc(gates_ready[b], 1)

            pe.wait_ge(lstm_in, 16 * 5)
            pe.wait_ge(gb_ready, 1)
            for b in range(2):
                for g in range(4):
                    gates_x(b, g, 0, 1)

            def pe_step(j, count, group):
                for b in range(2):
                    gates_h(b, j, count)
                    if group is not None:
                        gates_x(b, j % GROUP, 1 - j // GROUP, group)

            for st in range(UNROLL):
                pe_step(st, st + 1, st // GROUP + 2)
            with pe.Fori(1, NG // 2 - 1) as it:
                for st in range(UNROLL):
                    pe_step(st, it * UNROLL + (st + 1), it * 2 + (st // GROUP + 2))
            for st in range(UNROLL):
                pe_step(st, S - UNROLL + st + 1, NG if st < GROUP else None)
            def fuse(t):
                for a in range(2):
                    last = mm(ps[a][:, t * C:(t + 1) * C], dsc_s[:, a, t, :], f23_s[:, a, :], start=(t == 0), stop=(t == K - 1))
                    if t == K - 1:
                        last.then_inc(fuse_mm, 1)
                mm(ps[(2, 3, 6)[t // 4]][:, (t % 4) * P:(t % 4 + 1) * P], cw_s[:, t, :], fus_s, start=(t % 4 == 0),
                   stop=(t % 4 == 3))

            pe.wait_ge(conv_in, 16 * 6)
            pe.wait_ge(h_stored, 2 + NG - 1)
            pe.wait_ge(h_last, 1)
            for n in range(NCH):
                pe.wait_ge(x1_ready, 2 * n + 2)
                mm(ps[4 + n % 2], wlin_s, seq[:, n * 4 * SEQ:(n + 1) * 4 * SEQ], start=True, stop=True).then_inc(lin_ready, 1)
                if 1 <= n <= K:
                    fuse(n - 1)
            mm(ps[6][:, P:P + 1], fus_s, vecs[:, V_CONVB:V_CONVB + 1], start=False, stop=True).then_inc(fuse_mm, 1)
            norm_mm(GN2, 2)
            pe.wait_ge(fuse_ev, 3)
            def conv(b, lo, hi):
                pe.wait_ge(pad_ready[b], 1)
                with pe.Fori(lo, hi) as it:
                    for par in range(2):
                        pe.wait_ge(conv_ev, it * 2 + (8 * b + par + 1))
                        for t in range(9):
                            last = mm(ps[par], cwf[:, t, :], pad_rows(b, it * (2 * ROWS) + ROWS * par, t // 3, t % 3, ROWS),
                                      start=(t == 0), stop=(t == 8))
                        last.then_inc(conv_mm, 1)
            conv(0, 0, 4)
            conv(1, 0, CONV_SPLIT)
            norm_mm(BNX, 1)
            conv(1, CONV_SPLIT, 4)
            def part_wait(ready, ready_v, a, b, n):
                if a == 1 and n >= 2:
                    pe.wait_ge(ready_v, 2 * b + n - 1)
                elif a == 1:
                    pe.wait_ge(ready, 8 + 2 * b + n + 1)
                else:
                    pe.wait_ge(ready, 4 * b + n + 1)

            pe.wait_ge(conv_ev, 2 + NCH)
            pe.wait_ge(dmask_in, 16)
            for a in range(2):
                for b in range(2):
                    if a == 0 and b == 1:
                        pe.wait_ge(part3, NCH // 4)
                        norm_mm(BNY, 1)
                        pe.wait_ge(sqrt_in, BNY + 1)
                    if a == 0:
                        pe.wait_ge(relu_done, 2 * b + 2)
                    else:
                        pe.wait_ge(relu_v, b + 1)
                    for n in range(8):
                        if n % 2 == 0:
                            if a == 1 and b == 1:
                                part_wait(part3, part3_v, a, 0, n // 2)
                            elif a + b > 0:
                                pe.wait_ge(part3, 4 * a + n // 2 + 1)
                        r0 = slice(n * ROWS, (n + 1) * ROWS)
                        rhs = hv[a][:, b, r0, :] if a == 0 else hv[a][:, b, :, r0].rearrange("p h w -> p w h")
                        last = mm(ps[n][0:NROW, :], pws[:, a, :], rhs, start=True, stop=True)
                        if n % 2 == 1:
                            last.then_inc(off_mm, 1)
                    for m, (ready, ready_v, done) in enumerate(((part1, part1_v, rest1), (part2, part2_v, rest2))):
                        for n in range(8):
                            if n % 2 == 0:
                                part_wait(ready, ready_v, a, b, n // 2)
                            last = mm(ps[n][0:NROW, :], dmask[:, m, :],
                                      ob[a][0:ONE_ROW + 1, b * PIX + n * CH:b * PIX + (n + 1) * CH],
                                      start=False, stop=True, skip_group_check=True)
                            if n % 2 == 1:
                                last.then_inc(done, 1)
            def dist(s, slots, par, off, i):
                if not (isinstance(s, int) and (s + slots) * HATS + i < ND):
                    pe.wait_ge(d_read, s * HATS + (slots * HATS + i - ND + 1))
                for e in range(2):
                    k = 4 * Q + e if i == 8 else 4 * (2 * (i % 2) + e) + i // 2
                    last = mm(ps[D_BANK[i % ND]][:, e * SL:(e + 1) * SL], sels[:, k, :], offs[0:NROW, off],
                              start=(e == 0), stop=(e == 1))
                last.then_inc(d_ready, 1)

            def project(a, s, slots, par, q, r):
                x_r = xc[:, par, r * S:(r + 1) * S]
                if r == 0 and not (isinstance(s, int) and (s + slots) * Q + q < 2):
                    pe.wait_ge(y_read, s * Q + (slots * Q + q - 1))
                for e in range(2):
                    last = mm(ps[Y_BANK[q % 2]][S * e:S * e + S, r * P:(r + 1) * P], x_r, wm[:, a, q, e * P:(e + 1) * P],
                              start=(r == 0), stop=(r == HROWS - 1))
                if r == HROWS - 1:
                    last.then_inc(y_ready, 1)

            def project_last(a, s, slots, par, r):
                x_r = xc[:, par, r * S:(r + 1) * S]
                if r == 0 and not (isinstance(s, int) and s + slots < 1):
                    pe.wait_ge(y8_read, s + slots)
                for e in range(2):
                    last = mm(ps[Y8_BANK][S * e:S * e + S, r * 2 * C:(r + 1) * 2 * C], x_r, wm[:, a, e:Q:2, 2 * P:2 * P + C],
                              start=(r == 0), stop=(r == HROWS - 1))
                if r == HROWS - 1:
                    last.then_inc(y8_ready, 1)

            GROUPS = HROWS * 5
            STEPS = Q * HROWS
            LAST_TAP = 3
            LEAD = 4

            def product(par, group):
                r, k = group // 5, group % 5
                cols = slice(r * S, (r + 1) * S)
                for q in range(Q):
                    w, v = ((y8[:, par, q, r, :], v8[:, par, q // 2, cols]) if k == 4 else
                            (yt[:, par, q, r, k * C:(k + 1) * C], vt[:, par, k, q, cols]))
                    last = mm(ps[O_BANK[par]][C * q:C * q + C, cols], w, v, start=(group == 0), stop=(group == GROUPS - 1))
                if group == GROUPS - 1:
                    last.then_inc(out_ready, 1)

            def slot(a, s, slots, par, off):
                for i in range(STEPS):
                    if off is not None:
                        nslots = 0 if slots is None else slots + 1
                        if i == 0:
                            pe.wait_ge(xc_ready, s + (nslots + 1))
                        if i in HAT_STEP:
                            dist(s, nslots, 1 - par, off, HAT_STEP.index(i))
                        project(a, s, nslots, 1 - par, i // HROWS, i % HROWS)
                        if i % HROWS == LAST_TAP:
                            project_last(a, s, nslots, 1 - par, i // HROWS)
                    if slots is not None and i >= LEAD:
                        if i == LEAD:
                            pe.wait_ge(v_ready, s * HATS + (slots + 1) * HATS)
                            pe.wait_ge(y_read, s * Q + (slots + 1) * Q)
                            pe.wait_ge(y8_read, s + (slots + 1))
                            pe.wait_ge(out_read, s + (slots + 1))
                        j, n = i - LEAD, STEPS - LEAD
                        for group in range(j * GROUPS // n, (j + 1) * GROUPS // n):
                            product(par, group)

            pe.wait_ge(pos_in, 32)
            part_wait(part3, part3_v, 1, 1, 1)
            part_wait(part3, part3_v, 1, 1, 3)
            pe.wait_ge(wm_ready, 1)
            for a in range(2):
                s0 = 2 * a * NCH
                if a == 0:
                    slot(a, s0, None, 1, ds(0, SL))
                with pe.Fori(0, NCH - 1) as g:
                    for par in range(2):
                        slot(a, g * 2, s0 + par, par, ds(g * CH + (a * L + (par + 1) * SL), SL))
                slot(a, 2 * NCH - 2, s0, 0, ds(a * L + L - SL, SL))
                slot(1, 2 * NCH - 2, s0 + 1, 1, ds(L, SL) if a == 0 else None)
            norm_mm(BNF, 1)


def layout(inputs):
    import numpy as np
    f = np.float32
    g = {k: np.asarray(v) for k, v in inputs.items()}
    order = (2, 0, 1, 3)
    wx = np.zeros((P, 2, 4, DQ), f)
    whh = np.zeros((P, 4, P), f)
    wlin = np.zeros((P, P), f)
    gb = np.zeros((12, 2, P), f)
    for q in range(Q):
        for d, n in enumerate("fb"):
            hid = slice(q * HID, (q + 1) * HID)
            col = slice(d * DQ + q * HID, d * DQ + (q + 1) * HID)
            wih, wh = g[f"L0_conv_W_ih_{n}"], g[f"L0_conv_W_hh_{n}"]
            for j, t in enumerate(order):
                wx[q * 32:(q + 1) * 32, d, j, hid] = wih[t * HID:(t + 1) * HID].T
                whh[col, j, col] = wh[t * HID:(t + 1) * HID].T
                for p in range(PARTS):
                    gb[4 * p + j, 0, col] = g[f"L0_conv_b_ih_{n}"][t * HID:(t + 1) * HID]
                    gb[4 * p + j, 1, col] = g[f"L0_conv_b_hh_{n}"][t * HID:(t + 1) * HID]
            wlin[col, q * 32:(q + 1) * 32] = g["L0_conv_W_lin"][:, d * HID:(d + 1) * HID].T
    gi = np.zeros((12, 4 * GROUP * S), f)
    for p in range(PARTS):
        for j in range(4):
            gi[4 * p + j, j * GROUP * S:(j + 1) * GROUP * S] = 1
    cw = np.zeros((P, K, P), f)
    fus = np.zeros((P, P), f)
    fw = g["L1_conv_fus_w"][:, :, 0, 0]
    for q in range(Q):
        s = slice(q * 32, (q + 1) * 32)
        for t in range(9):
            cw[s, t, s] = g["L1_conv_conv_w"][:, :, t // 3, t % 3]
        fus[s, s] = fw[:, 0:32].T
    f23 = np.zeros((C, 3, C), f)
    f23[:, 0] = fw[:, 32:64].T
    f23[:, 1] = fw[:, 64:96].T
    dsc = np.zeros((C, 2, K, P), f)
    pw = np.zeros((P, 2, NROW), f)
    vec = np.zeros((P, NVEC), f)
    for a, n in enumerate("xy"):
        w = g[f"L1_conv_dsc{n}_w"]
        pww, pwb = g[f"L1_conv_off{n}_pw_w"][:, :, 0, 0], g[f"L1_conv_off{n}_pw_b"]
        for q in range(Q):
            s = slice(q * 32, (q + 1) * 32)
            for k in range(K):
                dsc[:, a, k, s] = w[:, :, k]
            for p in range(PARTS):
                r = p * NOFF + q * K
                pw[s, a, r:r + K] = pww.T
                vec[r:r + K, V_PWB + a] = pwb
            vec[s, V_DWB + a] = g[f"L1_conv_off{n}_dw_b"]
            vec[s, V_BNG + a] = g[f"L1_conv_off{n}_bn_g"]
            vec[s, V_BNB + a] = g[f"L1_conv_off{n}_bn_b"]
            vec[s, V_DW + 9 * a:V_DW + 9 * a + 9] = g[f"L1_conv_off{n}_dw_w"].reshape(C, 9)
        vec[ONE_ROW, V_PWB + a] = 1
    for q in range(Q):
        s = slice(q * 32, (q + 1) * 32)
        vec[s, V_BLIN] = g["L0_conv_b_lin"]
        vec[s, V_CONVB] = g["L1_conv_conv_b"]
        vec[s, V_FG] = g["L1_conv_fus_bn_g"]
        vec[s, V_FB] = g["L1_conv_fus_bn_b"]
    vec[4:12, V_G1] = -1
    vec[8:12, V_G2] = -1
    ch = np.arange(P)
    avg = np.zeros((P, 2, P), f)
    avg[:, 0] = 0.5 * (ch[:, None] // 2 == ch[None] // 2)
    avg[:, 1] = 0.25 * (ch[:, None] % C == ch[None] % C)
    sel = np.zeros((NROW, NSEL, P), f)
    for n in range(NSEL):
        for e in range(2):
            q, k = (n // 4, 2 * (n % 4) + e) if n < 4 * Q else (2 * (n - 4 * Q) + e, 8)
            for p in range(PARTS):
                sel[p * NOFF + q * K + k, n, e * S:(e + 1) * S] = 1
            sel[ONE_ROW, n, e * S:(e + 1) * S] = -np.arange(S)
            sel[ONE_ROW + 1, n, e * S:(e + 1) * S] = 1
    dm = np.zeros((ONE_ROW + 1, 2, NROW), f)
    for m in range(2):
        rows = np.arange((m + 1) * NOFF, ONE_ROW)
        dm[rows, m, rows] = -1
    pos = np.tile(np.arange(S), L // S)[None].astype(f)
    bits = lambda a: (a.view(np.uint32) >> 16).astype(np.uint16)
    return dict(x=g["x"], wx=wx, whh=whh, wlin=wlin, gate_bias=gb, gate_ind=bits(gi), cw=cw, fus=fus, f23=f23,
                dsc=dsc, pw=pw, dm=bits(dm), vec=vec, avg=avg, sel=bits(sel), pos=bits(pos))


def kernel(**inputs):
    import numpy as _np
    import concourse.bacc as _bacc
    from concourse import mybir as _mybir
    from concourse.bass_utils import run_bass_kernel_spmd as _run

    nc = _bacc.Bacc("TRN2", target_bir_lowering=False, num_devices=1)
    arrays, args = {}, {}
    for name, a in layout(inputs).items():
        a = _np.ascontiguousarray(a)
        arrays[f"in_{name}_dram"] = a
        args[name] = nc.dram_tensor(f"in_{name}_dram", a.shape, _mybir.dt.from_np(a.dtype), kind="ExternalInput").ap()
    args["fus"] = (args["fus"], args.pop("f23"))
    out = nc.dram_tensor("out_0_dram", (2 * Q, C, S, S), _mybir.dt.float32, kind="ExternalOutput").ap()
    build(nc, out=out, **args)
    r = _run(nc, [arrays], core_ids=[0])
    return r.results[0]["out_0_dram"]
```
